# Optimizing a Trainium2 kernel written in Bass

```python
import numpy as np
import jax
import jax.numpy as jnp

def _softmax(x, axis=-1):
    return jax.nn.softmax(x, axis=axis)

def _gelu(x):
    return jax.nn.gelu(x, approximate=True)

def _silu(x):
    return jax.nn.silu(x)

def _sigmoid(x):
    return jax.nn.sigmoid(x)

def _layernorm(x, axis=-1, eps=1e-05):
    m = jnp.mean(x, axis=axis, keepdims=True)
    v = jnp.var(x, axis=axis, keepdims=True)
    return (x - m) / jnp.sqrt(v + eps)

def _scatter_add(tgt, idx, src, axis=0):
    return tgt.at[idx].add(src)

def _segment_sum(src, seg, n):
    return jax.ops.segment_sum(src, seg, n)
kernel_name = 'mk_xattn_ffn_d2_seqx_r4_0bffa0'

def setup_inputs(seed: int=0):
    np.random.seed(seed)
    _w = jnp.asarray

    def _rec_inputs():
        import jax
        import jax.numpy as jnp
        _rk = jax.random.key(seed)
        x = -0.0003929 + 0.9999 * jax.random.normal(jax.random.fold_in(_rk, 1), (16, 128, 256), jnp.float32)
        _lenS = 128 - jax.random.randint(jax.random.fold_in(_rk, 7), (16,), 0, max(1, 128 // 4) + 1, jnp.int32)
        _lenS2 = 128 - jax.random.randint(jax.random.fold_in(_rk, 8), (16,), 0, max(1, 128 // 4) + 1, jnp.int32)
        _ctx_1024P = jax.random.normal(jax.random.fold_in(_rk, 11), (16, 16, 256), jnp.float32)
        _ctx_1024c = jax.random.dirichlet(jax.random.fold_in(_rk, 511), 0.3 * jnp.ones((16,), jnp.float32), (16, 128))
        _ctx_1024t = jnp.einsum('bsk,bkd->bsd', _ctx_1024c, _ctx_1024P)
        _ctx_1024t = _ctx_1024t * jax.lax.rsqrt(jnp.mean(jnp.square(_ctx_1024t)) + 1e-12) * 0.953939
        ctx_1024 = 2.81802e-05 + 1.00001 * (_ctx_1024t + 0.3 * jax.random.normal(jax.random.fold_in(_rk, 611), (16, 128, 256), jnp.float32))
        return (x, ctx_1024)
    x, ctx_1024 = _rec_inputs()

    def _L0_xattn_setup():
        import jax, jax.numpy as jnp
        import numpy as np
        B, L, D = (4, 1024, 256)
        key = jax.random.key(seed)
        k1, k2 = jax.random.split(key)
        Q = jax.random.normal(k1, (B, L, D), dtype=jnp.float32)
        K = jax.random.normal(k2, (B, L, D), dtype=jnp.float32)
        return {'Q': Q, 'K': K}
    _L0_xattn_all = _L0_xattn_setup()
    _L0_xattn_in = {k: v for k, v in _L0_xattn_all.items() if k in ()}
    del _L0_xattn_all

    def _L0_ffn_setup():
        import jax, jax.numpy as jnp
        import numpy as np
        B, S, D = (2, 256, 256)
        L, H = (128, 16)
        HD = L // H
        F, E, K = (512, 8, 2)
        THETA = 10000.0
        EPS = 1e-05

        def _rmsnorm(x, g):
            return x * g * jax.lax.rsqrt(jnp.mean(x * x, axis=-1, keepdims=True) + EPS)

        def _rope(t, pos):
            inv_freq = 1.0 / THETA ** (jnp.arange(0, HD, 2, dtype=jnp.float32) / HD)
            ang = pos[:, None].astype(jnp.float32) * inv_freq[None, :]
            cos, sin = (jnp.cos(ang), jnp.sin(ang))
            t1, t2 = (t[..., 0::2], t[..., 1::2])
            r1 = t1 * cos - t2 * sin
            r2 = t1 * sin + t2 * cos
            return jnp.stack([r1, r2], axis=-1).reshape(t.shape)

        def _forward(x, g1, g2, w_down, wq, wk, wv, w_up, router_w, w1, w2, w3):
            b, s, _ = x.shape
            pos = jnp.arange(s)
            h = _rmsnorm(x, g1)
            c = h @ w_down
            split = lambda t: t.reshape(b, s, H, HD).transpose(0, 2, 1, 3)
            q = _rope(split(c @ wq), pos)
            k = _rope(split(c @ wk), pos)
            v = split(c @ wv)
            scores = jnp.einsum('bhqd,bhkd->bhqk', q, k) / jnp.sqrt(jnp.float32(HD))
            causal = jnp.tril(jnp.ones((s, s), bool))
            scores = jnp.where(causal, scores, -jnp.inf)
            attn = jax.nn.softmax(scores, axis=-1)
            o = jnp.einsum('bhqk,bhkd->bhqd', attn, v).transpose(0, 2, 1, 3).reshape(b, s, L)
            x = x + o @ w_up
            res = x
            t = _rmsnorm(x, g2).reshape(-1, D)
            probs = jax.nn.softmax(t @ router_w, axis=-1)
            vals, idx = jax.lax.top_k(probs, K)
            w = vals / jnp.sum(vals, axis=-1, keepdims=True)
            gate = jnp.sum(jax.nn.one_hot(idx, E, dtype=t.dtype) * w[..., None], axis=1)
            hid = jax.nn.silu(jnp.einsum('td,edf->tef', t, w1)) * jnp.einsum('td,edf->tef', t, w3)
            y_e = jnp.einsum('tef,efd->ted', hid, w2)
            y = jnp.einsum('ted,te->td', y_e, gate)
            return res + y.reshape(b, s, D)
        key = jax.random.key(seed)
        ks = jax.random.split(key, 12)
        g = lambda k, shape, scale: jax.random.normal(k, shape, dtype=jnp.float32) * scale
        return {'x': g(ks[0], (B, S, D), 1.0), 'g1': jnp.ones((D,), jnp.float32), 'g2': jnp.ones((D,), jnp.float32), 'w_down': g(ks[1], (D, L), 0.02), 'wq': g(ks[2], (L, L), 0.02), 'wk': g(ks[3], (L, L), 0.02), 'wv': g(ks[4], (L, L), 0.02), 'w_up': g(ks[5], (L, D), 0.02), 'router_w': g(ks[6], (D, E), 0.02), 'w1': g(ks[7], (E, D, F), 0.02), 'w3': g(ks[8], (E, D, F), 0.02), 'w2': g(ks[9], (E, F, D), 0.02)}
    _L0_ffn_all = _L0_ffn_setup()
    _L0_ffn_in = {k: v for k, v in _L0_ffn_all.items() if k in ('g1', 'g2', 'w_down', 'wq', 'wk', 'wv', 'w_up', 'router_w', 'w1', 'w2', 'w3')}
    del _L0_ffn_all

    def _L1_xattn_setup():
        import jax, jax.numpy as jnp
        import numpy as np
        DIM = 256
        NUM_HEADS = 16
        DIM_HEAD = 64
        INNER = NUM_HEADS * DIM_HEAD
        SCALE = DIM_HEAD ** (-0.5)

        def _layernorm(x, gamma, beta, eps=1e-05):
            mu = jnp.mean(x, axis=-1, keepdims=True)
            var = jnp.mean(jnp.square(x - mu), axis=-1, keepdims=True)
            return (x - mu) * jax.lax.rsqrt(var + eps) * gamma + beta
        key = jax.random.key(seed)
        ks = jax.random.split(key, 8)
        B, SQ, SK = (2, 512, 1024)
        x = jax.random.normal(ks[0], (B, SQ, DIM), dtype=jnp.float32)
        context = jax.random.normal(ks[1], (B, SK, DIM), dtype=jnp.float32)
        ln_gamma = jnp.ones((DIM,), jnp.float32)
        ln_beta = jnp.zeros((DIM,), jnp.float32)
        w_q = jax.random.normal(ks[2], (DIM, INNER), dtype=jnp.float32) / np.sqrt(DIM)
        w_kv = jax.random.normal(ks[3], (DIM, 2 * INNER), dtype=jnp.float32) / np.sqrt(DIM)
        w_out = jax.random.normal(ks[4], (INNER, DIM), dtype=jnp.float32) / np.sqrt(INNER)
        b_out = jnp.zeros((DIM,), jnp.float32)
        gate = jnp.array([0.5], jnp.float32)
        return {'x': x, 'context': context, 'ln_gamma': ln_gamma, 'ln_beta': ln_beta, 'w_q': w_q, 'w_kv': w_kv, 'w_out': w_out, 'b_out': b_out, 'gate': gate}
    _L1_xattn_all = _L1_xattn_setup()
    _L1_xattn_in = {k: v for k, v in _L1_xattn_all.items() if k in ('ln_gamma', 'ln_beta', 'w_q', 'w_kv', 'w_out', 'b_out', 'gate')}
    del _L1_xattn_all

    def _L1_ffn_setup():
        import jax, jax.numpy as jnp
        import numpy as np
        D_MODEL = 256
        N_EXPERTS = 16
        TOP_K = 2
        EXPERT_DIM = 256
        SHARED_DIM = 512
        B, T = (2, 256)
        key = jax.random.key(seed)
        ks = jax.random.split(key, 7)
        std = 0.02
        return {'x': jax.random.normal(ks[0], (B, T, D_MODEL), dtype=jnp.float32), 'router_w': jax.random.normal(ks[1], (N_EXPERTS, D_MODEL), dtype=jnp.float32) * std, 'gate_up_w': jax.random.normal(ks[2], (N_EXPERTS, D_MODEL, 2 * EXPERT_DIM), dtype=jnp.float32) * std, 'down_w': jax.random.normal(ks[3], (N_EXPERTS, EXPERT_DIM, D_MODEL), dtype=jnp.float32) * std, 'shared_gate_w': jax.random.normal(ks[4], (SHARED_DIM, D_MODEL), dtype=jnp.float32) * std, 'shared_up_w': jax.random.normal(ks[5], (SHARED_DIM, D_MODEL), dtype=jnp.float32) * std, 'shared_down_w': jax.random.normal(ks[6], (D_MODEL, SHARED_DIM), dtype=jnp.float32) * std}
    _L1_ffn_all = _L1_ffn_setup()
    _L1_ffn_in = {k: v for k, v in _L1_ffn_all.items() if k in ('router_w', 'gate_up_w', 'down_w', 'shared_gate_w', 'shared_up_w', 'shared_down_w')}
    del _L1_ffn_all
    return {'x': x, 'ctx_1024': ctx_1024, 'L0_ffn_g1': _L0_ffn_in['g1'], 'L0_ffn_g2': _L0_ffn_in['g2'], 'L0_ffn_w_down': _L0_ffn_in['w_down'], 'L0_ffn_wq': _L0_ffn_in['wq'], 'L0_ffn_wk': _L0_ffn_in['wk'], 'L0_ffn_wv': _L0_ffn_in['wv'], 'L0_ffn_w_up': _L0_ffn_in['w_up'], 'L0_ffn_router_w': _L0_ffn_in['router_w'], 'L0_ffn_w1': _L0_ffn_in['w1'], 'L0_ffn_w2': _L0_ffn_in['w2'], 'L0_ffn_w3': _L0_ffn_in['w3'], 'L1_xattn_ln_gamma': _L1_xattn_in['ln_gamma'], 'L1_xattn_ln_beta': _L1_xattn_in['ln_beta'], 'L1_xattn_w_q': _L1_xattn_in['w_q'], 'L1_xattn_w_kv': _L1_xattn_in['w_kv'], 'L1_xattn_w_out': _L1_xattn_in['w_out'], 'L1_xattn_b_out': _L1_xattn_in['b_out'], 'L1_xattn_gate': _L1_xattn_in['gate'], 'L1_ffn_router_w': _L1_ffn_in['router_w'], 'L1_ffn_gate_up_w': _L1_ffn_in['gate_up_w'], 'L1_ffn_down_w': _L1_ffn_in['down_w'], 'L1_ffn_shared_gate_w': _L1_ffn_in['shared_gate_w'], 'L1_ffn_shared_up_w': _L1_ffn_in['shared_up_w'], 'L1_ffn_shared_down_w': _L1_ffn_in['shared_down_w']}

def reference(x, ctx_1024, L0_ffn_g1, L0_ffn_g2, L0_ffn_w_down, L0_ffn_wq, L0_ffn_wk, L0_ffn_wv, L0_ffn_w_up, L0_ffn_router_w, L0_ffn_w1, L0_ffn_w2, L0_ffn_w3, L1_xattn_ln_gamma, L1_xattn_ln_beta, L1_xattn_w_q, L1_xattn_w_kv, L1_xattn_w_out, L1_xattn_b_out, L1_xattn_gate, L1_ffn_router_w, L1_ffn_gate_up_w, L1_ffn_down_w, L1_ffn_shared_gate_w, L1_ffn_shared_up_w, L1_ffn_shared_down_w):
    import jax
    import jax.numpy as jnp

    def _L0_xattn_ref(Q, K):
        import jax, jax.numpy as jnp
        import numpy as np
        B, L, D = (4, 1024, 256)
        scores = jnp.einsum('btd,bsd->bts', K, K)
        Lq = Q.shape[1]
        mask = jnp.tril(jnp.ones((Lq, Lq), dtype=scores.dtype))
        scores = scores * mask[None, :, :]
        Q_proj = jnp.einsum('bts,bsd->btd', scores, Q)
        return Q + Q_proj

    def _L0_ffn_ref(x, g1, g2, w_down, wq, wk, wv, w_up, router_w, w1, w2, w3):
        import jax, jax.numpy as jnp
        import numpy as np
        B, S, D = (2, 256, 256)
        L, H = (128, 16)
        HD = L // H
        F, E, K = (512, 8, 2)
        THETA = 10000.0
        EPS = 1e-05

        def _rmsnorm(x, g):
            return x * g * jax.lax.rsqrt(jnp.mean(x * x, axis=-1, keepdims=True) + EPS)

        def _rope(t, pos):
            inv_freq = 1.0 / THETA ** (jnp.arange(0, HD, 2, dtype=jnp.float32) / HD)
            ang = pos[:, None].astype(jnp.float32) * inv_freq[None, :]
            cos, sin = (jnp.cos(ang), jnp.sin(ang))
            t1, t2 = (t[..., 0::2], t[..., 1::2])
            r1 = t1 * cos - t2 * sin
            r2 = t1 * sin + t2 * cos
            return jnp.stack([r1, r2], axis=-1).reshape(t.shape)

        def _forward(x, g1, g2, w_down, wq, wk, wv, w_up, router_w, w1, w2, w3):
            b, s, _ = x.shape
            pos = jnp.arange(s)
            h = _rmsnorm(x, g1)
            c = h @ w_down
            split = lambda t: t.reshape(b, s, H, HD).transpose(0, 2, 1, 3)
            q = _rope(split(c @ wq), pos)
            k = _rope(split(c @ wk), pos)
            v = split(c @ wv)
            scores = jnp.einsum('bhqd,bhkd->bhqk', q, k) / jnp.sqrt(jnp.float32(HD))
            causal = jnp.tril(jnp.ones((s, s), bool))
            scores = jnp.where(causal, scores, -jnp.inf)
            attn = jax.nn.softmax(scores, axis=-1)
            o = jnp.einsum('bhqk,bhkd->bhqd', attn, v).transpose(0, 2, 1, 3).reshape(b, s, L)
            x = x + o @ w_up
            res = x
            t = _rmsnorm(x, g2).reshape(-1, D)
            probs = jax.nn.softmax(t @ router_w, axis=-1)
            vals, idx = jax.lax.top_k(probs, K)
            w = vals / jnp.sum(vals, axis=-1, keepdims=True)
            gate = jnp.sum(jax.nn.one_hot(idx, E, dtype=t.dtype) * w[..., None], axis=1)
            hid = jax.nn.silu(jnp.einsum('td,edf->tef', t, w1)) * jnp.einsum('td,edf->tef', t, w3)
            y_e = jnp.einsum('tef,efd->ted', hid, w2)
            y = jnp.einsum('ted,te->td', y_e, gate)
            return res + y.reshape(b, s, D)
        return _forward(x, g1, g2, w_down, wq, wk, wv, w_up, router_w, w1, w2, w3)

    def _L1_xattn_ref(x, context, ln_gamma, ln_beta, w_q, w_kv, w_out, b_out, gate):
        import jax, jax.numpy as jnp
        import numpy as np
        DIM = 256
        NUM_HEADS = 16
        DIM_HEAD = 64
        INNER = NUM_HEADS * DIM_HEAD
        SCALE = DIM_HEAD ** (-0.5)

        def _layernorm(x, gamma, beta, eps=1e-05):
            mu = jnp.mean(x, axis=-1, keepdims=True)
            var = jnp.mean(jnp.square(x - mu), axis=-1, keepdims=True)
            return (x - mu) * jax.lax.rsqrt(var + eps) * gamma + beta
        B, SQ, _ = x.shape
        SK = context.shape[1]
        xn = _layernorm(x, ln_gamma, ln_beta)
        q = (xn @ w_q).reshape(B, SQ, NUM_HEADS, DIM_HEAD)
        kv = context @ w_kv
        k, v = jnp.split(kv, 2, axis=-1)
        k = k.reshape(B, SK, NUM_HEADS, DIM_HEAD)
        v = v.reshape(B, SK, NUM_HEADS, DIM_HEAD)
        scores = jnp.einsum('bqhd,bkhd->bhqk', q * SCALE, k)
        attn = jax.nn.softmax(scores, axis=-1)
        out = jnp.einsum('bhqk,bkhd->bqhd', attn, v).reshape(B, SQ, INNER)
        out = out @ w_out + b_out
        return out * jnp.tanh(gate[0])

    def _L1_ffn_ref(x, router_w, gate_up_w, down_w, shared_gate_w, shared_up_w, shared_down_w):
        import jax, jax.numpy as jnp
        import numpy as np
        D_MODEL = 256
        N_EXPERTS = 16
        TOP_K = 2
        EXPERT_DIM = 256
        SHARED_DIM = 512
        B, T = (2, 256)
        Bb, Tt, C = x.shape
        N = Bb * Tt
        E = gate_up_w.shape[0]
        logits = jnp.einsum('btc,ec->bte', x, router_w)
        top_vals, top_idx = jax.lax.top_k(logits, TOP_K)
        gates = jax.nn.sigmoid(top_vals)
        xf = x.reshape(N, C)
        sel = top_idx.reshape(N, TOP_K)
        gw = gates.reshape(N, TOP_K)
        w_full = jnp.zeros((N, E), dtype=x.dtype).at[jnp.arange(N)[:, None], sel].add(gw)
        gu = jnp.einsum('nc,ech->neh', xf, gate_up_w)
        gate, up = jnp.split(gu, 2, axis=-1)
        h = jax.nn.silu(gate) * up
        out_all = jnp.einsum('neh,ehc->nec', h, down_w)
        moe = jnp.einsum('ne,nec->nc', w_full, out_all).reshape(Bb, Tt, C)
        sg = jnp.einsum('btc,sc->bts', x, shared_gate_w)
        su = jnp.einsum('btc,sc->bts', x, shared_up_w)
        shared = jnp.einsum('bts,cs->btc', jax.nn.silu(sg) * su, shared_down_w)
        return moe + shared
    x = x + _L0_xattn_ref(_layernorm(x, axis=-1), ctx_1024)
    x = x + _L0_ffn_ref(_layernorm(x, axis=-1), L0_ffn_g1, L0_ffn_g2, L0_ffn_w_down, L0_ffn_wq, L0_ffn_wk, L0_ffn_wv, L0_ffn_w_up, L0_ffn_router_w, L0_ffn_w1, L0_ffn_w2, L0_ffn_w3)
    x = x + _L1_xattn_ref(_layernorm(x, axis=-1), ctx_1024, L1_xattn_ln_gamma, L1_xattn_ln_beta, L1_xattn_w_q, L1_xattn_w_kv, L1_xattn_w_out, L1_xattn_b_out, L1_xattn_gate)
    x = x + _L1_ffn_ref(_layernorm(x, axis=-1), L1_ffn_router_w, L1_ffn_gate_up_w, L1_ffn_down_w, L1_ffn_shared_gate_w, L1_ffn_shared_up_w, L1_ffn_shared_down_w)
    return x

_drawn_inputs = setup_inputs


def setup_inputs(seed=0):
    import zlib

    import numpy as np

    out = dict(_drawn_inputs(seed))
    spreads = {'L0_ffn_g1': (1.0, 0.6),
     'L0_ffn_g2': (1.0, 0.6),
     'L1_xattn_ln_gamma': (1.0, 0.6),
     'L1_xattn_ln_beta': (0.0, 0.8),
     'L1_xattn_b_out': (0.0, 2.0)}
    factors = {'L0_ffn_w_down': 8.0,
     'L0_ffn_wq': 8.0,
     'L0_ffn_wk': 8.0,
     'L0_ffn_wv': 8.0,
     'L0_ffn_w_up': 8.0,
     'L0_ffn_router_w': 8.0,
     'L0_ffn_w1': 8.0,
     'L0_ffn_w2': 8.0,
     'L0_ffn_w3': 8.0,
     'L1_xattn_w_q': 8.0,
     'L1_xattn_w_kv': 8.0,
     'L1_xattn_w_out': 8.0,
     'L1_ffn_router_w': 21.622,
     'L1_ffn_gate_up_w': 8.0,
     'L1_ffn_down_w': 8.0,
     'L1_ffn_shared_gate_w': 21.788,
     'L1_ffn_shared_up_w': 8.0,
     'L1_ffn_shared_down_w': 8.0}
    for name, (base, spread) in spreads.items():
        noise = np.random.default_rng([zlib.crc32(name.encode()), seed]).standard_normal(out[name].shape)
        drawn = base * np.exp(spread * noise) if base else spread * noise
        out[name] = jnp.asarray(drawn.astype(out[name].dtype))
    for name, factor in factors.items():
        out[name] = (out[name] * factor).astype(out[name].dtype)
    return out
```

```python
from contextlib import ExitStack
from functools import partial

import numpy as np
import concourse.bass as bass
from concourse import mybir

F32 = mybir.dt.float32
BF16 = mybir.dt.bfloat16
I32 = mybir.dt.int32
U32 = mybir.dt.uint32
ALU = mybir.AluOpType
ACT = mybir.ActivationFunctionType
AX = mybir.AxisListType.X

NB = 16
D = 256
EPS = 1e-5
H0, HD0 = 16, 8
E0, F0 = 8, 512
E1, F1 = 16, 256
H1, HD1 = 16, 64
CAP = 2048 + 128
NT0 = 32 + E0 - 1
NT1 = 32 + E1 - 1
KB = 256
BIGKB = 154

CONST = {}
_at = 0
for _name, _n in (("ident", 128), ("triu", 128), ("strict", 128), ("neg", 128), ("rc", 8), ("rs", 4),
                  ("hmask", 16), ("iota0", 2 * E0), ("iota1", 2 * E1), ("ecap0", E0), ("ecap1", E1),
                  ("cmp", 16), ("j", 1), ("j128", 1), ("mhalf", 1)):
    CONST[_name] = (_at, _n)
    _at += _n
NCONST = _at


def constants():
    c = np.zeros((128, NCONST), np.float32)

    def put(name, a):
        o, n = CONST[name]
        c[:, o:o + n] = np.broadcast_to(np.asarray(a, np.float32), (128, n))

    p = np.arange(128)
    put("ident", np.eye(128))
    put("triu", p[:, None] <= p[None, :])
    put("strict", p[:, None] < p[None, :])
    put("neg", np.where(p[None, :] > p[:, None], -1e30, 0.0))
    inv = np.float32(1.0) / np.float32(10000.0) ** (np.arange(0, HD0, 2, dtype=np.float32) / np.float32(HD0))
    ang = p[:, None].astype(np.float32) * inv[None, :].astype(np.float32)
    cos, sin = np.cos(ang).astype(np.float32), np.sin(ang).astype(np.float32)
    put("rc", np.repeat(cos, 2, axis=1))
    put("rs", sin)
    put("hmask", p[:, None] // HD0 == np.arange(16)[None, :])
    put("iota0", np.tile(np.arange(E0), 2))
    put("iota1", np.tile(np.arange(E1), 2))
    put("ecap0", np.arange(E0) * CAP)
    put("ecap1", np.arange(E1) * CAP)
    put("cmp", np.arange(16) * 128)
    put("j", p[:, None])
    put("mhalf", -0.5)
    put("j128", p[:, None] * 128)
    return c


class Queue:

    def __init__(self, name):
        self.name, self.ops, self.t = name, [], 0.0


class Ring:

    def __init__(self, tiles, first=()):
        self.tiles, self.left, self.free = tiles, [list(first) for _ in tiles], list(range(len(tiles)))
        self.asked, self.served = 0, 0

    def give(self, i, *tokens):
        assert i not in self.free
        self.free.append(i)
        self.left[i] = list(tokens)


class Weave:

    def __init__(self, when):
        self.when, self.live, self.age = when, [], 0

    def spawn(self, gen):
        done = []
        self.live.append([[], self.age, gen, done])
        return lambda: bool(done)

    def run(self, gens, depth, slope):
        todo, n = list(gens), 0
        while todo or self.live:
            while todo and sum(1 for e in self.live if len(e) == 5) < depth:
                self.live.append([[], n, todo.pop(0), [], True])
                n += 1
            best = None
            for e in self.live:
                if callable(e[0]):
                    if not e[0]():
                        continue
                    e[0] = []
                key = self.when(e[0]) + slope * e[1]
                if best is None or key < best[0]:
                    best = (key, e)
            assert best, "no generator can go on"
            e = best[1]
            self.age = e[1]
            want = next(e[2], "end")
            if want == "end":
                e[3].append(True)
                self.live.remove(e)
            else:
                e[0] = want if callable(want) else [want]


def program(nc, a, out):
    with ExitStack() as ctx:
        sems = {}

        def sem(name):
            if name not in sems:
                sems[name] = [ctx.enter_context(nc.semaphore(name)), 0]
            return sems[name]

        pe, dve, act, pool, sp = (Queue(n) for n in ("s_pe", "s_dve", "s_act", "s_pool", "s_sp"))

        def flat(ws):
            for w in ws:
                if w is None:
                    continue
                if isinstance(w, list) or not isinstance(w[0], str):
                    yield from flat(w)
                else:
                    yield w

        expected, line = {}, Queue("line")
        DELAY = {"s_pe": 90, "s_dve": 130, "s_act": 60, "s_pool": 60}

        def when(ws):
            return max([expected.get(w, 0.0) for w in flat(ws)], default=0.0)

        def price(q, fn):
            if not isinstance(fn, partial):
                return 100.0
            name = fn.func.__name__
            n = max(int(np.prod(v.shape[1:])) for v in (*fn.args, *fn.keywords.values()) if isinstance(v, bass.AP))
            if q is pe:
                if name == "transpose":
                    return 107.0
                n = int(np.prod(fn.args[0].shape[1:]))
                return max(n, 64) * (0.42 if fn.args[2].dtype == BF16 else 1.67)
            if q is dve:
                return 67 + n * 1.044
            if q is act:
                return 51 + n * 0.834 + (186 if "accum_out" in fn.keywords else 0)
            return 464.0 if ALU.pow in fn.args else 150 + n * 2.1

        def spend(q, fn, waits, ns=None):
            q.t = max(q.t, when(waits)) + (price(q, fn) if ns is None else ns)
            return q.t

        def op(q, fn, *waits, ns=None):
            s = sem(q.name)
            s[1] += 1
            q.ops.append((waits, fn, (q.name, 1)))
            expected[(q.name, s[1])] = spend(q, fn, waits, ns) + DELAY[q.name]
            return (q.name, s[1])

        def quiet(q, fn, *waits, ns=None):
            q.ops.append((waits, fn, None))
            spend(q, fn, waits, ns)

        def dma(q, name, dst, src, *waits, fn=None):
            s = sem(name)
            s[1] += 16
            q.ops.append((waits, fn or (lambda e: e.dma_start(dst, src)), (name, 16)))
            size = 4 * int(np.prod(dst.shape)) if fn is None else 4 * 128 * D
            line.t = max(line.t, spend(q, None, waits, 1040 if q is pool else 60)) + size / 180
            expected[(name, s[1])] = line.t + 2000
            return (name, s[1])

        weave = Weave(when)
        spawn = weave.spawn

        def grab(ring):
            turn = ring.asked
            ring.asked += 1
            if ring.served < turn or not ring.free:
                yield lambda: ring.served == turn and bool(ring.free)
            ring.served += 1
            i = min(ring.free, key=lambda i: when(ring.left[i]))
            ring.free.remove(i)
            yield ring.left[i]
            return i, ring.tiles[i], ring.left[i]

        def play(q, e):
            seen = {}
            for waits, fn, inc in q.ops:
                need = {}
                for name, v in flat(waits):
                    need[name] = max(need.get(name, 0), v)
                for name, v in need.items():
                    if seen.get(name, 0) < v:
                        e.wait_ge(sems[name][0], v)
                        seen[name] = v
                r = fn() if isinstance(fn, partial) else fn(e)
                if inc:
                    r.then_inc(sems[inc[0]][0], inc[1])

        def sb(name, shape, dt=F32):
            return ctx.enter_context(nc.sbuf_tensor(name, shape, dt))

        X = sb("X", [128, NB, D])
        CT = sb("CT", [128, NB, 2, 128])
        TT = [sb(f"TT{i}", [128, D]) for i in range(3)]
        BIG = sb("BIG", [128, BIGKB * KB])
        W0, XW0, WK0 = 0, 96 * KB, 128 * KB
        CS = sb("CS", [128, NCONST])
        cst = {k: CS[:, o:o + n] for k, (o, n) in CONST.items()}
        identb = sb("identb", [128, 128], BF16)
        strictb = sb("strictb", [128, 128], BF16)
        onesb = sb("onesb", [128, 128], BF16)
        negb = sb("negb", [128, 128], BF16)
        st = sb("st", [128, 8, 16])
        zero = sb("zero", [128, D])
        v8 = sb("v8", [128, NB, 8])
        i8 = sb("i8", [128, NB, 8], U32)
        OH = sb("OH", [128, NB, 2, E1], BF16)
        CNT = sb("CNT", [128, NB + 1, E1])
        PF = sb("PF", [128, NB, 2])
        PI = sb("PI", [128, NB, 2], I32)
        YI = sb("YI", [128, NB, 2], I32)
        GW = sb("GW", [128, NB, 2])
        RT = sb("RT", [128, 4, 32])
        RC = sb("RC", [128, 8 * 32])
        TI = sb("TI", [128, 2], I32)
        sc = sb("sc", [128, 40])
        ident, ident_f = cst["ident"], cst["ident"]

        bank_t = [ctx.enter_context(nc.psum_tensor(f"ps{i}", [128, 512], F32)) for i in range(8)]
        banks = Ring(bank_t)
        XS = nc.dram_tensor("xs_dram", [E1 * CAP, D], F32, kind="Internal").ap()
        YS = nc.dram_tensor("ys_dram", [NT1 * 128, D], F32, kind="Internal").ap()

        def big(at_kb, cnt, **kw):
            v = BIG[:, int(at_kb * KB):int(at_kb * KB) + cnt]
            if kw:
                pat = kw.pop("pat")
                v = v.rearrange(pat, **kw)
            return v

        small = sb("small", [128, 256 + 384 + 256 + 2 * E0 + 256 + 2])
        xv = a["x"].rearrange("b p f -> p b f")
        t_x = []
        for g in range(4):
            t = dma(sp, f"d_x{g}", X[:, 4 * g:4 * g + 4, :], xv[:, 4 * g:4 * g + 4, :])
            t_x += [t] * 4
            if g == 0:
                t_cst = dma(sp, "d_cst", CS[:, :], a["consts"])
                t_ct0 = dma(sp, "d_ct0", CT[:, 0:4, :, :], a["ctxT"][:, 0:4, :, :])
                t_small = dma(sp, "d_small", small[:, :], a["small0"])
        t_ct1 = dma(sp, "d_ct1", CT[:, 4:NB, :, :], a["ctxT"][:, 4:NB, :, :])
        wdn = small[:, 0:256].rearrange("p (k n) -> p k n", k=2)
        wqkv = small[:, 256:640]
        wup = small[:, 640:896]
        rt0 = small[:, 896:912].rearrange("p (k n) -> p k n", k=2)
        g2b = small[:, 912:1168]
        g1c = small[:, 1168:1170]

        WGU0 = big(0, 64 * KB)
        WD0 = big(64, 32 * KB)
        t_w0 = [dma(sp, "d_wgu0", WGU0, a["wgu0"]), dma(sp, "d_wd0", WD0, a["wd0"])]

        t_k = [op(act, partial(nc.scalar.copy, identb[:, :], ident), t_cst),
               op(act, partial(nc.scalar.copy, strictb[:, :], cst["strict"]), t_cst),
               op(act, partial(nc.scalar.copy, negb[:, :], cst["neg"]), t_cst),
               op(dve, partial(nc.vector.memset, onesb[:, :], 1.0)),
               op(dve, partial(nc.vector.memset, zero[:, :], 0.0))]
        t_rc = op(dve, partial(nc.vector.memset, RC[:, :], 0.0))
        t_wdn = [op(act, partial(nc.scalar.mul, wdn[:, k, :], wdn[:, k, :], g1c[:, k:k + 1]), t_small)
                 for k in range(2)]

        stat = Ring([st[:, i, :] for i in range(8)])

        def rsqrt(dst, src, *ready):
            t = op(dve, partial(nc.vector.tensor_scalar, dst, src, EPS, None, ALU.add), *ready)
            yield t
            t = op(pool, partial(nc.gpsimd.tensor_tensor, dst, dst, cst["mhalf"], ALU.pow), t, t_cst)
            yield t
            return t

        def layernorm(src, dst, *ready):
            i, s, free = yield from grab(stat)
            yield list(ready)
            t = op(dve, partial(nc.vector.bn_stats, s[:, 0:6], src), list(ready), free)
            t = op(dve, partial(nc.vector.bn_aggr, s[:, 6:8], s[:, 0:6]), t)
            t = yield from rsqrt(s[:, 8:9], s[:, 7:8], t)
            t = op(dve, partial(nc.vector.tensor_scalar, dst, src, s[:, 6:7], s[:, 8:9], ALU.subtract, ALU.mult), t)
            stat.give(i, t)
            yield t
            return t

        def transposes(src, n, *ready):
            yield list(ready)
            i, bk, free = yield from grab(banks)
            for k in range(n):
                f = partial(nc.tensor.transpose, bk[:, k * 128:(k + 1) * 128], src[:, k * 128:(k + 1) * 128], ident)
                if k < n - 1:
                    quiet(pe, f, list(ready), free, t_cst)
                else:
                    t = op(pe, f, list(ready), free, t_cst)
            yield t
            return i, bk, t

        def mm(o, l, r, start, stop, last, *waits):
            f = partial(nc.tensor.matmul, o, l, r, start=start, stop=stop)
            if last:
                return op(pe, f, *waits)
            quiet(pe, f, *waits)

        def evac(q, dst, src, *waits):
            if q is act:
                return op(act, partial(nc.scalar.copy, dst, src), *waits)
            return op(dve, partial(nc.vector.tensor_copy, dst, src), *waits)

        class Route:
            pass

        def route_tile(R, b, logits_bank, t_log, itt, tt, t_tt):
            E, bi, bk = R.E, *logits_bank
            il, lg, f = yield from grab(R.rt)
            lg = lg[:, 0:E]
            yield t_log
            t = op(dve, partial(nc.vector.tensor_copy, lg, bk[:, 0:E]), t_log, f)
            banks.give(bi, t)
            t1 = op(dve, partial(nc.vector.max, v8[:, b, :], lg), t, R.v8free)
            t2 = op(dve, partial(nc.vector.max_index, i8[:, b, :], v8[:, b, :], lg), t1, R.v8free)
            R.v8.append(t2)
            t = op(dve, partial(nc.vector.tensor_copy, PF[:, b, :], i8[:, b, 0:2]), t2, R.pffree)
            oh = OH[:, b, :, 0:E]
            t_oh = op(dve, partial(nc.vector.tensor_tensor, oh, cst[R.iota].rearrange("p (k n) -> p k n", k=2),
                                   PF[:, b, :].rearrange("p (k o) -> p k o", o=1).broadcast_to([128, 2, E]),
                                   ALU.is_equal), t, R.ohfree)
            im, m, f = yield from grab(R.mb)
            m = m[:, 0:E]
            t_m = op(dve, partial(nc.vector.tensor_tensor, m, oh[:, 0, :], oh[:, 1, :], ALU.add), t_oh, f)
            yield t_m
            pi_, pb, free = yield from grab(banks)
            mm(pb[:, 0:E], strictb[:, :], m, True, True, False, t_m, free, t_k)
            t_r = mm(pb[:, E:2 * E], onesb[:, :], m, True, True, True)
            R.mb.give(im, t_r)
            ir, pr, f = yield from grab(R.pr)
            pr = pr[:, 0:2 * E].rearrange("p (k n) -> p k n", k=2)
            yield t_r
            n = R.n
            R.n += 1
            t_p = op(dve, partial(nc.vector.tensor_tensor, lg, pb[:, 0:E], CNT[:, n, 0:E], ALU.add), t_r, t2, R.cnt)
            R.cnt = op(dve, partial(nc.vector.tensor_tensor, CNT[:, n + 1, 0:E], pb[:, E:2 * E], CNT[:, n, 0:E], ALU.add),
                       t_r, R.cnt)
            banks.give(pi_, R.cnt)
            t_q = op(dve, partial(nc.vector.tensor_tensor, pr, oh, lg.rearrange("p (o n) -> p o n", o=1)
                                  .broadcast_to([128, 2, E]), ALU.mult), t_p, f)
            R.rt.give(il, t_q)
            t_f = op(dve, partial(nc.vector.tensor_reduce, PF[:, b, :], pr, AX, ALU.add), t_q, t_oh)
            R.pr.give(ir, t_f)
            t_i = op(dve, partial(nc.vector.tensor_copy, PI[:, b, :], PF[:, b, :]), t_f, R.pifree)
            R.pf.append(t_f)
            yield t_i
            for k in range(2):
                t = dma(pool, f"d_sc{itt}", None, None, t_i, t_tt, R.xsfree, t_k,
                        fn=partial(nc.gpsimd.indirect_dma_start, XS,
                                   bass.IndirectOffsetOnAxis(ap=PI[:, b, k:k + 1], axis=0), tt[:, :], None))
            R.scat.append(t)
            return t

        def route_start(E, names, prev):
            R = Route()
            R.E, R.NT, R.n = E, 32 + E - 1, 0
            R.iota, R.ecap = names
            R.rt = Ring([RT[:, i, :] for i in range(4)], [prev])
            R.mb = Ring([m[:, :] for m in mb0], [prev])
            R.pr = Ring([pr0[:, i, :] for i in range(2)], [prev])
            R.pf, R.scat, R.v8 = [], [], []
            R.v8free = R.pffree = R.ohfree = R.pifree = R.xsfree = prev
            R.cnt = op(dve, partial(nc.vector.tensor_copy, CNT[:, 0, 0:E], cst[R.ecap]), t_cst, prev)
            return R

        def route_end(R):
            E = R.E
            t_pad = op(dve, partial(nc.vector.tensor_copy, R.pad, CNT[:, NB, 0:E]), R.cnt)
            for x in range(E):
                def pad(e, x=x):
                    v = e.value_load(R.pad[0:1, x:x + 1], min_val=0, max_val=E * CAP - 128)
                    return e.dma_start(XS[bass.ds(v, 128), :], zero[:, :])
                dma((sp, act)[x % 2], f"d_pad{x % 2}", None, None, t_pad, t_k, R.xsfree, fn=pad)
            R.tpad = [(f"d_pad{i}", sem(f"d_pad{i}")[1]) for i in range(2)]
            RC3 = R.ohw.rearrange("p a n -> p (a n)")[:, 0:E * 16].rearrange("p (n j) -> p n j", n=E)
            buf = [RC[:, 32 * i:32 * i + 32] for i in range(6)]
            nn, nt, of, w1 = sc[:, 0:E], sc[:, 16:16 + E], RC[:, 192:192 + E], RC[:, 224:224 + E]
            t = op(dve, partial(nc.vector.tensor_tensor, nn, CNT[:, NB, 0:E], cst[R.ecap], ALU.subtract), R.cnt, R.scfree)
            t = op(dve, partial(nc.vector.tensor_tensor, RC3, nn.rearrange("p (n o) -> p n o", o=1)
                                                  .broadcast_to([128, E, 16]),
                                                  cst["cmp"].rearrange("p (o j) -> p o j", o=1)
                                                  .broadcast_to([128, E, 16]), ALU.is_gt),
                   t, t_rc, R.tifree, R.ohwfree)
            t = t_cmp = op(dve, partial(nc.vector.tensor_reduce, nt, RC3, AX, ALU.add), t)
            t_nt = t
            t = op(dve, partial(nc.vector.tensor_copy, buf[0][:, 16:16 + E], nt), t)
            k, i = 1, 0
            while k < E:
                t = op(dve, partial(nc.vector.tensor_tensor, buf[i + 1][:, 16:16 + E], buf[i][:, 16:16 + E],
                                                                buf[i][:, 16 - k:16 - k + E], ALU.add), t)
                k, i = 2 * k, i + 1
            inc = buf[i][:, 16:16 + E]
            t_of = op(dve, partial(nc.vector.tensor_tensor, of, nt, inc, ALU.subtract), t, t_nt)
            t_of = op(dve, partial(nc.vector.scalar_tensor_tensor, out=of, in0=of, scalar=128.0, in1=cst[R.ecap],
                                                            op0=ALU.mult, op1=ALU.add), t_of)
            t = op(dve, partial(nc.vector.tensor_scalar, w1, inc, cst["j"], None, ALU.is_le), t)
            te, va, r = sc[:, 32:33], sc[:, 33:34], sc[:, 34:35]
            t = op(dve, partial(nc.vector.tensor_reduce, te, w1, AX, ALU.add), t)
            t_va = op(dve, partial(nc.vector.tensor_scalar, va, te, float(E), None, ALU.is_lt), t)
            t = op(dve, partial(nc.vector.tensor_tensor, te, te, va, ALU.mult), t_va)
            t_te = t
            t = op(dve, partial(nc.vector.tensor_scalar, w1, cst[R.iota][:, 0:E], te, None, ALU.is_equal), t)
            t = op(dve, partial(nc.vector.tensor_tensor, w1, w1, of, ALU.mult), t, t_of)
            t = op(dve, partial(nc.vector.tensor_reduce, r, w1, AX, ALU.add), t)
            t = op(dve, partial(nc.vector.tensor_scalar, r, r, cst["j128"], va, ALU.add, ALU.mult), t, t_va)
            t1 = op(dve, partial(nc.vector.tensor_copy, TI[:, 0:1], te), t_te, R.tifree)
            R.ti = op(dve, partial(nc.vector.tensor_copy, TI[:, 1:2], r), t, R.tifree)
            OHw = R.ohw
            oh = OH[:, :, :, 0:E].rearrange("p b k n -> p (b k) n")
            t = op(dve, partial(nc.vector.tensor_tensor, OHw, oh, of.rearrange("p (o n) -> p o n", o=1)
                                                  .broadcast_to([128, 2 * NB, E]), ALU.mult), t_of, t_cmp, R.ohwfree)
            y1 = R.y1
            t = op(dve, partial(nc.vector.tensor_reduce, y1, OHw, AX, ALU.add), t)
            t = op(dve, partial(nc.vector.tensor_tensor, y1, PF[:, :, :].rearrange("p b k -> p (b k)"), y1, ALU.subtract),
                   t, R.pf)
            R.yi = op(dve, partial(nc.vector.tensor_copy, YI[:, :, :].rearrange("p b k -> p (b k)"), y1), t, R.yifree)

        mb0 = [sb(f"mb{i}", [128, E1], BF16) for i in range(2)]
        pr0 = sb("pr0", [128, 2, 32])

        RS = 96
        off = [XW0 // KB]

        def ring(n, cols, first=()):
            tiles = []
            for _ in range(n):
                tiles.append(BIG[:, int(off[0] * KB):int(off[0] * KB) + cols])
                off[0] += cols / KB
            assert off[0] <= BIGKB, off
            return Ring(tiles, first)

        r_h = ring(6, D)
        r_v0 = ring(4, 16 * 9)
        r_qkT = ring(4, 256)
        r_o = ring(4, 128)
        r_rs = ring(6, 8)
        for i, v in enumerate(r_v0.tiles):
            ones = v.rearrange("p (h d) -> p h d", d=9)[:, :, 8:9]
            r_v0.left[i] = [op(dve, partial(nc.vector.memset, ones, 1.0))]
        r_q0 = ring(2, D)
        r_a = ring(2, 128)
        r_hn = ring(2, D)
        r_hnT = ring(3, D)
        r_tT = r_hnT
        r_cT = ring(2, 128)
        r_qk = ring(2, 256)
        r_m = ring(2, 256)
        r_oT = ring(2, 128)
        r_r = ring(2, D)
        r_sq = ring(1, D)
        r_km = ring(3, 512)
        r_p = ring(4, 512)
        r_pt = ring(4, 512)
        r_sm = ring(8, 16)
        r_tt = Ring(TT)
        PADI = sb("PADI", [128, E1], I32)
        Y1 = sb("Y1", [128, 2 * NB])
        KMACT = 2
        SC0 = float(np.float32(1.0) / np.sqrt(np.float32(HD0)))

        R0 = route_start(E0, ("iota0", "ecap0"), None)
        R0.scfree = None
        R0.pad, R0.y1, R0.tifree, R0.ohwfree, R0.yifree = PADI[:, 0:E0], Y1[:, :], None, None, None
        res_done = {}

        def latent_tile(b):
            x = X[:, b, :]
            tct = t_ct0 if b < 4 else t_ct1
            irs, rs, f_rs = yield from grab(r_rs)
            iq, q0, f = yield from grab(r_q0)
            t_q0 = yield from layernorm(x, q0, t_x[b], f)
            t_xq = op(pool, partial(nc.gpsimd.tensor_tensor, x, x, q0, ALU.add), t_q0)
            ia, A, f_a = yield from grab(r_a)
            yield tct
            bi, bk, f = yield from grab(banks)
            for k in range(2):
                t = mm(bk[:, 0:128], CT[:, b, k, :], CT[:, b, k, :], k == 0, k == 1, k == 1, tct, f)
            yield t
            t_a = op(dve, partial(nc.vector.tensor_tensor, A, bk[:, 0:128], cst["triu"], ALU.mult), t, f_a, t_cst)
            banks.give(bi, t_a)
            yield t_a
            bi, bk, f = yield from grab(banks)
            t = mm(bk[:, 0:D], A, q0, True, True, True, t_a, t_q0, f)
            r_a.give(ia, t)
            r_q0.give(iq, t, t_xq)
            yield t, t_xq
            t_x1 = op(dve, partial(nc.vector.tensor_tensor, x, bk[:, 0:D], x, ALU.add), t, t_xq)
            banks.give(bi, t_x1)
            ih, h, f = yield from grab(r_h)
            t_h = yield from layernorm(x, h, t_x1, f)
            isq, sq, f = yield from grab(r_sq)
            t = op(act, partial(nc.scalar.activation, sq, h, ACT.Square, scale=1.0 / 16, accum_out=rs[:, 0:1]),
                   t_h, f, f_rs)
            r_sq.give(isq, t)
            yield t
            t = yield from rsqrt(rs[:, 1:2], rs[:, 0:1], t)
            ihn, hn, f = yield from grab(r_hn)
            t_hn = op(act, partial(nc.scalar.mul, hn, h, rs[:, 1:2]), t, f)
            iT, hnT, f = yield from grab(r_hnT)
            bi, bk, t = yield from transposes(hn, 2, t_hn)
            r_hn.give(ihn, t)
            t_hnT = evac(act, hnT, bk[:, 0:D], t, f)
            banks.give(bi, t_hnT)
            ic, cT, f_c = yield from grab(r_cT)
            yield t_hnT
            bi, bk, f = yield from grab(banks)
            for k in range(2):
                t = mm(bk[:, 0:128], wdn[:, k, :], hnT[:, k * 128:(k + 1) * 128], k == 0, k == 1, k == 1,
                       t_hnT, t_wdn, f)
            r_hnT.give(iT, t)
            yield t
            t_cT = evac(act, cT, bk[:, 0:128], t, f_c)
            banks.give(bi, t_cT)
            iv, v, f_v = yield from grab(r_v0)
            ik, qkT, f_k = yield from grab(r_qkT)
            io, o_, f_o = yield from grab(r_o)
            iqk, qk, f_q = yield from grab(r_qk)
            im, m, f_m = yield from grab(r_m)
            yield t_cT
            bi, bk, f = yield from grab(banks)
            t = mm(bk[:, 0:384], cT, wqkv, True, True, True, t_cT, t_small, f)
            r_cT.give(ic, t)
            yield t
            t_v = evac(act, v.rearrange("p (h d) -> p h d", d=9)[:, :, 0:8],
                       bk[:, 256:384].rearrange("p (h d) -> p h d", d=8), t, f_v)
            t_qk = evac(act, qk, bk[:, 0:256], t, f_q)
            banks.give(bi, t_qk)
            yield t_qk
            rsb = cst["rs"].rearrange("p (o n) -> p o n", o=1).broadcast_to([128, 32, 4])
            rcb = cst["rc"].rearrange("p (o n) -> p o n", o=1).broadcast_to([128, 32, 8])
            q8 = qk.rearrange("p (h n) -> p h n", h=32)
            qv = qk.rearrange("p (h n two) -> p h n two", h=32, two=2)
            mv = m.rearrange("p (h n two) -> p h n two", h=32, two=2)
            t2 = op(pool, partial(nc.gpsimd.tensor_tensor, mv[:, :, :, 0], qv[:, :, :, 1], rsb, ALU.mult), t_qk, f_m, t_cst)
            t3 = op(pool, partial(nc.gpsimd.tensor_tensor, mv[:, :, :, 1], qv[:, :, :, 0], rsb, ALU.mult), t_qk, f_m)
            t1 = op(pool, partial(nc.gpsimd.tensor_tensor, q8, q8, rcb, ALU.mult), t2, t3)
            yield t1
            q2 = qk.rearrange("p (n two) -> p n two", two=2)
            m2 = m.rearrange("p (n two) -> p n two", two=2)
            t4 = op(dve, partial(nc.vector.tensor_tensor, q2[:, :, 0], q2[:, :, 0], m2[:, :, 0], ALU.subtract), t1)
            t5 = op(dve, partial(nc.vector.tensor_tensor, q2[:, :, 1], q2[:, :, 1], m2[:, :, 1], ALU.add), t1)
            r_m.give(im, t4, t5)
            bi, bk, t = yield from transposes(qk, 2, t4, t5)
            r_qk.give(iqk, t)
            t_qkT = evac(act, qkT, bk[:, 0:256], t, f_k)
            banks.give(bi, t_qkT)
            yield t_qkT
            t_o, used = [], []
            for k in [spawn(latent_heads(g, qkT, t_qkT, v, t_v, o_, f_o, t_o, used)) for g in range(4)]:
                yield k
            r_v0.give(iv, used)
            r_qkT.give(ik, used)
            iT, oT, f_t = yield from grab(r_oT)
            bi, bk, t = yield from transposes(o_, 1, t_o)
            r_o.give(io, t)
            t_oT = evac(act, oT, bk[:, 0:128], t, f_t)
            banks.give(bi, t_oT)
            ir, r, f_r = yield from grab(r_r)
            yield t_oT
            bi, bk, f = yield from grab(banks)
            t = mm(bk[:, 0:D], oT, wup, True, True, True, t_oT, t_small, f)
            r_oT.give(iT, t)
            yield t
            t_r = op(dve, partial(nc.vector.tensor_tensor, r, bk[:, 0:D], h, ALU.add), t, t_h, f_r)
            banks.give(bi, t_r)
            r_h.give(ih, t_r)
            isq, sq, f = yield from grab(r_sq)
            yield t_r
            t = op(act, partial(nc.scalar.activation, sq, r, ACT.Square, scale=1.0 / 16, accum_out=rs[:, 2:3]), t_r, f)
            r_sq.give(isq, t)
            yield t
            t = yield from rsqrt(rs[:, 3:4], rs[:, 2:3], t)
            itt, tt, f = yield from grab(r_tt)
            t_tt = op(dve, partial(nc.vector.scalar_tensor_tensor, out=tt[:, :], in0=r, scalar=rs[:, 3:4], in1=g2b,
                                   op0=ALU.mult, op1=ALU.mult), t, t_small, f)
            r_rs.give(irs, t_tt)
            t_xr = op(pool, partial(nc.gpsimd.tensor_tensor, x, x, r, ALU.add), t_r, t_h)
            r_r.give(ir, t_tt, t_xr)
            res_done[b] = t_xr
            iT, tT, f = yield from grab(r_tT)
            bi, bk, t = yield from transposes(tt, 2, t_tt)
            t_tT = evac(act, tT, bk[:, 0:D], t, f)
            t_ttpe = t
            banks.give(bi, t_tT)
            yield t_tT
            bi, bk, f = yield from grab(banks)
            for k in range(2):
                t = mm(bk[:, 0:E0], tT[:, k * 128:(k + 1) * 128], rt0[:, k, :], k == 0, k == 1, k == 1,
                       t_tT, t_small, f)
            r_tT.give(iT, t)
            t_sc = yield from route_tile(R0, b, (bi, bk), t, itt, tt, t_tt)
            r_tt.give(itt, t_sc, t_ttpe)

        def latent_heads(g, qkT, t_qkT, v, t_v, o_, f_o, t_o, used):
            kTb = qkT[:, 128:256].rearrange("p (o n) -> p o n", o=1).broadcast_to([128, 4, 128])
            ikm, km, f = yield from grab(r_km)
            hm = cst["hmask"][:, 4 * g:4 * g + 4].rearrange("p (n o) -> p n o", o=1).broadcast_to([128, 4, 128])
            if g < KMACT:
                for n in range(4):
                    t_km = op(act, partial(nc.scalar.mul, km[:, n * 128:(n + 1) * 128], qkT[:, 128:256],
                                           cst["hmask"][:, 4 * g + n:4 * g + n + 1]), t_qkT, f)
            else:
                t_km = op(dve, partial(nc.vector.tensor_tensor, km.rearrange("p (n t) -> p n t", n=4), kTb, hm, ALU.mult),
                          t_qkT, f)
            ism, sm, f_sm = yield from grab(r_sm)
            ip, p, f_p = yield from grab(r_p)
            yield t_km
            bi, bk, f = yield from grab(banks)
            mm(bk[:, :].rearrange("p (n t) -> p n t", n=4), identb[:, :],
               negb[:, :].rearrange("p (o t) -> p o t", o=1).broadcast_to([128, 4, 128]), True, False, False, f, t_k)
            t_s = mm(bk[:, :], qkT[:, 0:128], km, False, True, True, t_km, t_qkT)
            r_km.give(ikm, t_s)
            used += [t_s, t_km]
            yield t_s
            t = op(dve, partial(nc.vector.tensor_reduce, sm[:, 0:4], bk[:, :].rearrange("p (n t) -> p n t", n=4), AX,
                                ALU.max), t_s, f_sm)
            t_nm = op(dve, partial(nc.vector.tensor_scalar, sm[:, 4:8], sm[:, 0:4], -SC0, None, ALU.mult), t)
            yield t_nm
            for n in range(4):
                t_e = op(act, partial(nc.scalar.activation, p[:, n * 128:(n + 1) * 128], bk[:, n * 128:(n + 1) * 128],
                                      ACT.Exp, bias=sm[:, 4 + n:5 + n], scale=SC0), t_nm, f_p)
            banks.give(bi, t_e)
            ipt, pt, f = yield from grab(r_pt)
            yield t_e
            bi, bk, t = yield from transposes(p, 4, t_e)
            r_p.give(ip, t)
            t_pt = evac(act, pt, bk[:, :], t, f)
            banks.give(bi, t_pt)
            yield t_pt
            bi, bk, f = yield from grab(banks)
            for n in range(4):
                hh = 4 * g + n
                t = mm(bk[:, n * 9:n * 9 + 9], pt[:, n * 128:(n + 1) * 128],
                       v[:, hh * 9:hh * 9 + 9], True, True, n == 3, t_pt, t_v, f)
            used.append(t)
            r_pt.give(ipt, t)
            yield t
            og = o_[:, 32 * g:32 * g + 32].rearrange("p (n d) -> p n d", n=4)
            pv = bk[:, 0:36].rearrange("p (n d) -> p n d", n=4)
            sums = sm[:, 8:12].rearrange("p (n o) -> p n o", o=1)
            t_r = op(dve, partial(nc.vector.reciprocal, sums, pv[:, :, 8:9]), t)
            t = op(dve, partial(nc.vector.tensor_tensor, og, pv[:, :, 0:8], sums.broadcast_to([128, 4, 8]), ALU.mult),
                   t_r, f_o)
            banks.give(bi, t)
            r_sm.give(ism, t)
            t_o.append(t)

        weave.run((latent_tile(b) for b in range(NB)), 8, 100.0)

        def now():
            return [(n, sem(n)[1]) for n in ("s_pe", "s_dve", "s_act", "s_pool")]

        R0.ohw = big(152, 2 * NB * E0, pat="p (a n) -> p a n", n=E0)
        R0.ohwfree = now()
        route_end(R0)

        def gates(R, sigmoid):
            g = GW[:, :, :]
            if sigmoid:
                t = op(act, partial(nc.scalar.activation, g, v8[:, :, 0:2], ACT.Exp, scale=-1.0), R.v8, R.gwfree)
                t = op(dve, partial(nc.vector.tensor_scalar, g, g, 1.0, None, ALU.add), t)
                return op(dve, partial(nc.vector.reciprocal, g, g), t)
            t = op(dve, partial(nc.vector.tensor_tensor, GW[:, :, 1], v8[:, :, 1], v8[:, :, 0], ALU.subtract), R.v8)
            t = op(act, partial(nc.scalar.activation, GW[:, :, 1], GW[:, :, 1], ACT.Exp), t)
            t = op(dve, partial(nc.vector.tensor_scalar, GW[:, :, 0], GW[:, :, 1], 1.0, None, ALU.add), t)
            t = op(dve, partial(nc.vector.reciprocal, GW[:, :, 0], GW[:, :, 0]), t)
            return op(dve, partial(nc.vector.tensor_tensor, GW[:, :, 1], GW[:, :, 1], GW[:, :, 0], ALU.mult), t)

        R0.gwfree = None
        R0.gw = gates(R0, False)
        end0 = now()

        WQ = big(96, 8 * KB, pat="p (k n) -> p k n", k=2)
        WKV = big(104, 16 * KB, pat="p (k n) -> p k n", k=2)
        WO = big(120, 8 * KB, pat="p (c n) -> p c n", c=8)
        small1 = sb("small1", [128, 2 + 2 + 256 + 1 + 32])
        gam, bet, bo, gt = small1[:, 0:2], small1[:, 2:4], small1[:, 4:260], small1[:, 260:261]
        rt1 = small1[:, 261:293].rearrange("p (k n) -> p k n", k=2)
        loaded = {}

        def load_attention():
            loaded["wkv"] = dma(sp, "d_wkv", big(104, 16 * KB), a["wkv1"], end0)
            loaded["s1"] = dma(sp, "d_s1", small1[:, :], a["small1"])
            loaded["wq"] = dma(sp, "d_wq", big(96, 8 * KB), a["wq1"], end0)
            loaded["wo"] = dma(sp, "d_wo", big(120, 8 * KB), a["wo1"], end0)

        def experts(R, rings, wgu, wdn_, F, t_w, done, others=(), also=lambda: None):
            r_xs, r_xT, r_sg, r_hid, r_hT, r_y = rings
            E, K2 = R.E, F // 128

            def tile(j):
                ixs, xs, f = yield from grab(r_xs)

                def load(e):
                    v = e.value_load(TI[j:j + 1, 1:2], min_val=0, max_val=E * CAP - 128)
                    return e.dma_start(xs, XS[bass.ds(v, 128), :])
                t = dma(sp, f"d_xs{ixs}", None, None, R.ti, R.scat, R.tpad, f, fn=load)
                if j == 6:
                    also()
                iT, xT, f = yield from grab(r_xT)
                bi, bk, t = yield from transposes(xs, 2, t)
                r_xs.give(ixs, t)
                t_xT = evac(act, xT, bk[:, 0:D], t, f)
                banks.give(bi, t_xT)
                isg, sg, f_sg = yield from grab(r_sg)
                ihd, hid, f_hd = yield from grab(r_hid)
                yield t_xT
                ig, gk, f1 = yield from grab(banks)
                iu, uk, f2 = yield from grab(banks)
                ex = {}
                n = 2 * F

                def first(e):
                    ex["r"] = e.value_load(TI[j:j + 1, 0:1], min_val=0, max_val=E - 1)
                    return e.matmul(gk[:, 0:F], xT[:, 0:128], wgu[:, bass.ds(ex["r"] * (2 * n), F)],
                                    start=True, stop=False)

                quiet(pe, first, t_xT, f1, f2, R.ti, t_w, ns=F * 1.67)

                def part(o_, k, c, last):
                    f = lambda e: e.matmul(o_[:, 0:F], xT[:, k * 128:(k + 1) * 128],
                                           wgu[:, bass.ds(ex["r"] * (2 * n) + (k * n + c * F), F)],
                                           start=(k == 0), stop=(k == 1))
                    if last:
                        return op(pe, f, ns=F * 1.67)
                    quiet(pe, f, ns=F * 1.67)
                t_g = part(gk, 1, 0, True)
                part(uk, 0, 1, False)
                t_u = part(uk, 1, 1, True)
                r_xT.give(iT, t_u)
                yield t_g
                t_sg = op(act, partial(nc.scalar.activation, sg, gk[:, 0:F], ACT.Silu), t_g, f_sg)
                banks.give(ig, t_sg)
                yield t_u, t_sg
                t_h = op(dve, partial(nc.vector.tensor_tensor, hid, uk[:, 0:F], sg, ALU.mult), t_u, t_sg, f_hd)
                banks.give(iu, t_h)
                r_sg.give(isg, t_h)
                iT, hT, f = yield from grab(r_hT)
                bi, bk, t = yield from transposes(hid, K2, t_h)
                r_hid.give(ihd, t)
                t_hT = evac(act if j % 2 else dve, hT, bk[:, 0:F], t, f)
                banks.give(bi, t_hT)
                iy, y, f_y = yield from grab(r_y)
                yield t_hT
                bi, bk, f = yield from grab(banks)
                for k in range(K2):
                    fn = lambda e, k=k, bk=bk: e.matmul(bk[:, 0:D], hT[:, k * 128:(k + 1) * 128],
                                                        wdn_[:, bass.ds(ex["r"] * (K2 * D) + k * D, D)],
                                                        start=(k == 0), stop=(k == K2 - 1))
                    if k < K2 - 1:
                        quiet(pe, fn, t_hT, f, ns=D * 1.67)
                    else:
                        t = op(pe, fn, ns=D * 1.67)
                r_hT.give(iT, t)
                yield t
                t_y = evac(dve, y, bk[:, 0:D], t, f_y)
                banks.give(bi, t_y)
                yield t_y
                t = dma(sp, f"d_y{iy}", YS[j * 128:(j + 1) * 128, :], y, t_y, R.ysfree)
                r_y.give(iy, t)
                done[iy] = t

            weave.run([*others] + [tile(j) for j in range(R.NT)], 8, 100.0)

        off[0] = WK0 // KB
        rings0 = [ring(4, D, end0), ring(3, D, end0), ring(2, F0, end0), ring(2, F0, end0), ring(2, F0, end0),
                  ring(3, D, end0)]
        kv_at = off[0]
        R0.ysfree = None
        done0 = {}
        experts(R0, rings0, WGU0, WD0, F0, t_w0, done0, also=load_attention)
        t_wq, t_wkv, t_wo, t_s1 = (loaded[k] for k in ("wq", "wkv", "wo", "s1"))
        ys0 = list(done0.values())
        end1 = now()
        xs0 = [(f"d_xs{i}", sem(f"d_xs{i}")[1]) for i in range(4)]

        WGU1, WD1 = big(0, 64 * KB), big(64, 32 * KB)
        t_w1, t_ws, kv_done = [], [], []

        tg = sb("tg", [128, 1])
        btg = sb("btg", [128, D])
        t_tg = op(act, partial(nc.scalar.activation, tg[:, :], gt, ACT.Tanh), t_s1)
        t_btg = op(dve, partial(nc.vector.tensor_scalar, btg[:, :], bo, tg[:, 0:1], None, ALU.mult), t_tg, t_s1)

        G = [None]

        def gathered(R, b, ys):
            ig, g, f = yield from grab(G[0])
            g = g.rearrange("p (k n) -> p k n", k=2)
            yield R.yi, ys
            for k in range(2):
                t_g = dma(pool, f"d_g{ig}", None, None, R.yi, ys, f,
                          fn=partial(nc.gpsimd.indirect_dma_start, g[:, k, :], None, YS[0:R.NT * 128, :],
                                     bass.IndirectOffsetOnAxis(ap=YI[:, b, k:k + 1], axis=0)))
            yield t_g
            return ig, g, t_g

        def combine(R, b, got, *ready):
            ig, g, t_g = got
            x = X[:, b, :]
            t = op(dve, partial(nc.vector.scalar_tensor_tensor, out=x, in0=g[:, 0, :], scalar=GW[:, b, 0:1], in1=x,
                                                         op0=ALU.mult, op1=ALU.add), t_g, R.gw, *ready)
            t = op(dve, partial(nc.vector.scalar_tensor_tensor, out=x, in0=g[:, 1, :], scalar=GW[:, b, 1:2], in1=x,
                                                         op0=ALU.mult, op1=ALU.add), t)
            G[0].give(ig, t)
            return t

        off[0], off2 = WK0 // KB, [48]
        wk_free = [end1, ys0]

        def ring2(n, cols):
            tiles = []
            for _ in range(n):
                if off[0] * KB + cols <= BIGKB * KB:
                    at, off[0] = off[0], off[0] + cols / KB
                else:
                    at, off2[0] = off2[0], off2[0] + cols / KB
                assert off2[0] <= 96, off2
                tiles.append(BIG[:, int(at * KB):int(at * KB) + cols])
            return Ring(tiles, wk_free)

        r_kT = ring2(7, 512)
        r_v = ring2(7, 512)
        r_qT = ring2(3, 512)
        r_aT = ring2(3, 512)
        r_p1 = ring2(5, 512)
        G[0] = ring2(2, 512)
        r_pt1 = ring2(5, 512)
        r_xn = ring2(2, D)
        r_h1 = ring2(2, D)
        r_xnT = ring2(4, D)
        r_sm1 = ring2(8, 16)
        SC1 = float(HD1 ** -0.5)
        R1 = route_start(E1, ("iota1", "ecap1"), [end1, R0.gw, R0.yi, R0.scat, R0.tpad, xs0])
        R1.scfree = None
        t_hT = {}
        x4 = {}

        KVS, XNS, XT = {}, {}, {}

        def keys_values(b, u):
            ik, kT, f_k = yield from grab(r_kT)
            iv, v, f_v = yield from grab(r_v)
            yield t_wkv, f_k
            bi, bk, fb = yield from grab(banks)
            for c in range(4):
                cc = 4 * u + c
                for k in range(2):
                    t = mm(bk[:, c * 128:(c + 1) * 128], WKV[:, k, cc * 128:(cc + 1) * 128], CT[:, b, k, :],
                           k == 0, k == 1, c == 3 and k == 1, fb, t_wkv)
            yield t
            t_kT = evac(act, kT, bk[:, :], t, f_k)
            banks.give(bi, t_kT)
            bi, bk, fb = yield from grab(banks)
            for k in range(2):
                t = mm(bk[:, :], CT[:, b, k, :], WKV[:, k, 1024 + u * 512:1536 + u * 512],
                       k == 0, k == 1, k == 1, fb)
            yield t
            t_v = evac(dve, v, bk[:, :], t, f_v)
            banks.give(bi, t_v)
            KVS[b, u] = ik, kT, t_kT, iv, v, t_v, t
            kv_done.append(t)

        def attend(b, u, g, kT, t_kT, qT, t_q, pts, used):
            p0 = g * 64
            ism, sm, f_sm = yield from grab(r_sm1)
            ip, p, f_p = yield from grab(r_p1)
            yield t_q, t_kT
            bi, bk, f = yield from grab(banks)
            for n in range(4):
                t_s = mm(bk[:, n * 128:(n + 1) * 128], qT[p0:p0 + 64, n * 128:(n + 1) * 128],
                         kT[p0:p0 + 64, n * 128:(n + 1) * 128], True, True, n == 3, t_q, t_kT, f)
            used.append(t_s)
            yield t_s
            t = op(dve, partial(nc.vector.tensor_reduce, sm[:, 0:4],
                                bk[:, :].rearrange("p (n t) -> p n t", n=4), AX, ALU.max), t_s, f_sm)
            t_nm = op(dve, partial(nc.vector.tensor_scalar, sm[:, 4:8], sm[:, 0:4], -1.0, None, ALU.mult), t)
            yield t_nm
            for n in range(4):
                t_e = op(act, partial(nc.scalar.activation, p[:, n * 128:(n + 1) * 128],
                                      bk[:, n * 128:(n + 1) * 128], ACT.Exp, bias=sm[:, 4 + n:5 + n],
                                      accum_out=sm[:, 8 + n:9 + n]), t_nm, f_p)
            banks.give(bi, t_e)
            yield t_e
            t = op(dve, partial(nc.vector.reciprocal, sm[:, 12:16], sm[:, 8:12]), t_e)
            pv = p.rearrange("p (n t) -> p n t", n=4)
            t_p = op(dve, partial(nc.vector.tensor_tensor, pv, pv, sm[:, 12:16].rearrange("p (n o) -> p n o", o=1)
                                  .broadcast_to([128, 4, 128]), ALU.mult), t)
            r_sm1.give(ism, t_p)
            ipt, pt, f = yield from grab(r_pt1)
            bi, bk, t = yield from transposes(p, 4, t_p)
            r_p1.give(ip, t)
            t_pt = evac(act if g % 2 else dve, pt, bk[:, :], t, f)
            banks.give(bi, t_pt)
            pts[g] = ipt, pt, t_pt

        def heads(b, u):
            x = X[:, b, :]
            yield lambda: (b, u) in KVS and b in XNS
            ik, kT, t_kT, iv, v, t_v, _ = KVS[b, u]
            xnT, t_n = XNS[b]
            iq, qT, f_q = yield from grab(r_qT)
            yield t_n, t_wq
            bi, bk, fb = yield from grab(banks)
            for c in range(4):
                cc = 4 * u + c
                for k in range(2):
                    t = mm(bk[:, c * 128:(c + 1) * 128], WQ[:, k, cc * 128:(cc + 1) * 128],
                           xnT[:, k * 128:(k + 1) * 128], k == 0, k == 1, c == 3 and k == 1, fb, t_wq, t_n)
            t_xn = t
            yield t
            t_q = op(act, partial(nc.scalar.mul, qT, bk[:, :], SC1), t, f_q)
            banks.give(bi, t_q)
            pts, used = {}, []
            for k in [spawn(attend(b, u, g, kT, t_kT, qT, t_q, pts, used)) for g in range(2)]:
                yield k
            r_kT.give(ik, used)
            r_qT.give(iq, used)
            ia, aT, f_a = yield from grab(r_aT)
            yield pts[0][2], pts[1][2], t_v
            bi, bk, f = yield from grab(banks)
            for half in range(2):
                ipt, pt, t_pt = pts[half]
                for n in range(4):
                    t = mm(bk[half * 64:half * 64 + 64, n * 128:(n + 1) * 128],
                           v[:, (2 * n + half) * 64:(2 * n + half) * 64 + 64],
                           pt[:, n * 128:(n + 1) * 128], True, True, n == 3, t_pt, t_v, f)
                r_pt1.give(ipt, t)
            r_v.give(iv, t)
            yield t
            t_a = evac(act, aT, bk[:, :], t, f_a)
            banks.give(bi, t_a)
            yield t_a
            bi, bk, f = yield from grab(banks)
            for c in range(4):
                t = mm(bk[:, 0:D], aT[:, c * 128:(c + 1) * 128], WO[:, 4 * u + c, :], c == 0, c == 3, c == 3,
                       t_a, t_wo, f)
            r_aT.give(ia, t)
            yield t, XT[b]
            XT[b] = op(dve, partial(nc.vector.scalar_tensor_tensor, out=x, in0=bk[:, 0:D], scalar=tg[:, 0:1], in1=x,
                                    op0=ALU.mult, op1=ALU.add), t, XT[b], t_tg)
            banks.give(bi, XT[b])
            KVS[b, u] = t_xn, KVS[b, u][-1]

        def cross_tile(b):
            x = X[:, b, :]
            got = yield from gathered(R0, b, ys0)
            t_x = combine(R0, b, got, res_done[b])
            if b == 3:
                t_w1.append(dma(sp, "d_wgu1", big(0, 48 * KB), a["wgu1"][:, 0:48 * KB], end1))
            ih, h, f = yield from grab(r_h1)
            t = yield from layernorm(x, h, t_x, f)
            ixn, xn, f = yield from grab(r_xn)
            t_xn = yield from layernorm(h, xn, t, f)
            r_h1.give(ih, t_xn)
            XT[b] = op(pool, partial(nc.gpsimd.tensor_tensor, x, x, btg[:, :], ALU.add), t_x, t_xn, t_btg)
            iT, xnT, f = yield from grab(r_xnT)
            bi, bk, t = yield from transposes(xn, 2, t_xn)
            r_xn.give(ixn, t)
            for k in range(2):
                t_n = op(dve, partial(nc.vector.tensor_scalar, xnT[:, k * 128:(k + 1) * 128],
                                      bk[:, k * 128:(k + 1) * 128], gam[:, k:k + 1], bet[:, k:k + 1],
                                      ALU.mult, ALU.add), t, f, t_s1)
            banks.give(bi, t_n)
            XNS[b] = xnT, t_n
            for k in [spawn(heads(b, u)) for u in range(2)]:
                yield k
            r_xnT.give(iT, KVS[b, 0][0], KVS[b, 1][0])
            if b == NB - 1:
                t_ws.append(dma(sp, "d_wsg", big(104, 8 * KB), a["wsgu"], kv_done))
                t_ws.append(dma(sp, "d_wsd", big(112, 4 * KB), a["wsd"], kv_done))
            itt, tt, f = yield from grab(r_tt)
            t_tt = yield from layernorm(x, tt[:, :], XT[b], f)
            x4[b] = t_tt
            bi, bk, t = yield from transposes(tt, 2, t_tt)
            hT = CT[:, b, :, :].rearrange("p k t -> p (k t)")
            t_hT[b] = evac(act, hT, bk[:, 0:D], t, KVS[b, 0][1], KVS[b, 1][1])
            t_ttpe = t
            banks.give(bi, t_hT[b])
            yield t_hT[b]
            bi, bk, f = yield from grab(banks)
            for k in range(2):
                t = mm(bk[:, 0:E1], CT[:, b, k, :], rt1[:, k, :], k == 0, k == 1, k == 1, t_hT[b], t_s1, f)
            t_sc = yield from route_tile(R1, b, (bi, bk), t, itt, tt, t_tt)
            r_tt.give(itt, t_sc, t_ttpe)

        weave.run((g for b in range(NB) for g in (keys_values(b, 0), keys_values(b, 1), cross_tile(b))), 12, 100.0)
        end2 = now()
        WSG = big(104, 8 * KB, pat="p (k n) -> p k n", k=2)
        WSD = big(112, 4 * KB, pat="p (c n) -> p c n", c=4)
        t_w1 += [dma(sp, "d_wgu1", big(48, 16 * KB), a["wgu1"][:, 48 * KB:64 * KB], end2), dma(sp, "d_wd1", WD1, a["wd1"], end2)]
        R1.pad, R1.y1, R1.tifree = PADI[:, :], Y1[:, :], [R0.tpad, xs0, end1]
        R1.ohw, R1.ohwfree = big(152, 2 * NB * E1, pat="p (a n) -> p a n", n=E1), end2
        R1.yifree = [(f"d_g{i}", sem(f"d_g{i}")[1]) for i in range(2)]
        route_end(R1)
        R1.gwfree = end2
        R1.gw = gates(R1, True)

        r_hs = Ring([big(116, 2048), big(96, 2048)], end2)
        r_sg = Ring([big(124, 512), big(126, 512)], end2)

        def shared(s):
            ih, hs, f_h = yield from grab(r_hs)
            th = []
            for c in range(4):
                isg, sg, f_sg = yield from grab(r_sg)
                yield [t_hT[4 * s + i] for i in range(4)]
                ig, gk, f1 = yield from grab(banks)
                iu, uk, f2 = yield from grab(banks)
                for o_, w0, fb in ((gk, 0, f1), (uk, 512, f2)):
                    for k in range(2):
                        t = mm(o_[:, :].rearrange("p (b t) -> p b t", b=4), WSG[:, k, w0 + c * 128:w0 + (c + 1) * 128],
                               CT[:, 4 * s:4 * s + 4, k, :], k == 0, k == 1, k == 1, fb, t_ws,
                               [t_hT[4 * s + i] for i in range(4)])
                    if w0 == 0:
                        t_g = t
                yield t_g
                t_sg = op(act, partial(nc.scalar.activation, sg, gk[:, :], ACT.Silu), t_g, f_sg)
                banks.give(ig, t_sg)
                yield t, t_sg
                th.append(op(dve, partial(nc.vector.tensor_tensor, hs[:, c * 512:(c + 1) * 512], uk[:, :], sg, ALU.mult),
                             t, t_sg, f_h))
                banks.give(iu, th[-1])
                r_sg.give(isg, th[-1])
            yield th
            for i in range(4):
                b = 4 * s + i
                bi, bk, f = yield from grab(banks)
                for c in range(4):
                    t = mm(bk[:, 0:D], hs[:, c * 512 + i * 128:c * 512 + (i + 1) * 128], WSD[:, c, :], c == 0, c == 3,
                           c == 3, th, f)
                yield t
                x4[b] = op(dve, partial(nc.vector.tensor_tensor, X[:, b, :], bk[:, 0:D], X[:, b, :], ALU.add), t, x4[b])
                banks.give(bi, x4[b])
            r_hs.give(ih, t)

        off[0] = WK0 // KB
        rings1 = [ring(4, D, end2), ring(3, D, end2), ring(3, F1, end2), ring(3, F1, end2), ring(3, F1, end2),
                  ring(3, D, end2)]
        assert off[0] <= 152
        R1.ysfree = [(f"d_g{i}", sem(f"d_g{i}")[1]) for i in range(2)]
        done1 = {}
        experts(R1, rings1, WGU1, WD1, F1, t_w1, done1, others=(shared(0), shared(1)))
        G[0] = Ring([big(2 * i, 512) for i in range(NB)], now())
        ys1 = list(done1.values())

        outs, left = [], dict.fromkeys(range(NB), 1)
        left.update(dict.fromkeys(range(8, NB), 2))

        def finished(b):
            left[b] -= 1
            if not left[b]:
                yield x4[b]
                outs.append(dma(sp, "d_out", out[b], X[:, b, :], x4[b]))

        def last(b):
            got = yield from gathered(R1, b, ys1)
            x4[b] = combine(R1, b, got, x4[b])
            yield from finished(b)

        def shared_last(s):
            yield from shared(s)
            for b in range(4 * s, 4 * s + 4):
                yield from finished(b)

        weave.run([shared_last(2), shared_last(3)] + [last(b) for b in (*range(8, NB), *range(8))], 18, 0.0)
        quiet(sp, lambda e: e.nop(), outs[-1])

        block = ctx.enter_context(nc.Block())

        @block.sync
        def _(e):
            play(sp, e)

        @block.gpsimd
        def _(e):
            play(pool, e)

        @block.vector
        def _(e):
            play(dve, e)

        @block.scalar
        def _(e):
            play(act, e)

        @block.tensor
        def _(e):
            play(pe, e)


def laid_out(i):
    def kp(w):
        k, n = w.shape
        return w.reshape(k // 128, 128, n).transpose(1, 0, 2).reshape(128, -1)

    def ekp(w):
        e, k, n = w.shape
        return w.reshape(e, k // 128, 128, n).transpose(2, 0, 1, 3).reshape(128, -1)

    def rows(v):
        return np.broadcast_to(v.reshape(1, -1), (128, v.size))

    def cols(v):
        return v.reshape(-1, 128).T

    cat = np.concatenate
    d = {
        "consts": constants(),
        "x": i["x"],
        "ctxT": i["ctx_1024"].reshape(NB, 128, 2, 128).transpose(3, 0, 2, 1),
        "small0": cat([kp(i["L0_ffn_w_down"]), i["L0_ffn_wq"], i["L0_ffn_wk"], i["L0_ffn_wv"], i["L0_ffn_w_up"],
                       kp(i["L0_ffn_router_w"]), rows(i["L0_ffn_g2"]), cols(i["L0_ffn_g1"])], axis=1),
        "wgu0": ekp(cat([i["L0_ffn_w1"], i["L0_ffn_w3"]], axis=2)),
        "wd0": ekp(i["L0_ffn_w2"]),
        "wq1": kp(i["L1_xattn_w_q"]),
        "wkv1": kp(i["L1_xattn_w_kv"]),
        "wo1": kp(i["L1_xattn_w_out"]),
        "small1": cat([cols(i["L1_xattn_ln_gamma"]), cols(i["L1_xattn_ln_beta"]), rows(i["L1_xattn_b_out"]),
                       rows(i["L1_xattn_gate"]), kp(i["L1_ffn_router_w"].T)], axis=1),
        "wgu1": ekp(i["L1_ffn_gate_up_w"]),
        "wd1": ekp(i["L1_ffn_down_w"]),
        "wsgu": kp(cat([i["L1_ffn_shared_gate_w"].T, i["L1_ffn_shared_up_w"].T], axis=1)),
        "wsd": kp(i["L1_ffn_shared_down_w"].T),
    }
    return {k: np.ascontiguousarray(v) for k, v in d.items()}


def kernel(**inputs):
    import concourse.bacc as _bacc
    from concourse.bass_utils import run_bass_kernel_spmd as _run

    arrays = laid_out({k: np.asarray(v) for k, v in inputs.items()})
    nc = _bacc.Bacc("TRN2", target_bir_lowering=False, num_devices=1)
    args = {k: nc.dram_tensor(f"in_{k}", v.shape, mybir.dt.from_np(v.dtype), kind="ExternalInput").ap()
            for k, v in arrays.items()}
    out = nc.dram_tensor("out_dram", (NB, 128, D), F32, kind="ExternalOutput").ap()
    program(nc, args, out)
    r = _run(nc, [{f"in_{k}": v for k, v in arrays.items()}], core_ids=[0])
    return r.results[0]["out_dram"]
```

```python
from contextlib import ExitStack
from functools import partial

import numpy as np
import concourse.bass as bass
from concourse import mybir

F32 = mybir.dt.float32
F32R = mybir.dt.float32r
BF16 = mybir.dt.bfloat16
I32 = mybir.dt.int32
U32 = mybir.dt.uint32
ALU = mybir.AluOpType
ACT = mybir.ActivationFunctionType
AX = mybir.AxisListType.X

NB = 16
D = 256
EPS = 1e-5
H0, HD0 = 16, 8
E0, F0 = 8, 512
E1, F1 = 16, 256
H1, HD1 = 16, 64
CAP = 2048 + 128
NT0 = 32 + E0 - 1
NT1 = 32 + E1 - 1
KB = 256
BIGKB = 154

CONST = {}
_at = 0
for _name, _n in (("ident", 128), ("triu", 128), ("strict", 128), ("neg", 128), ("rc", 8), ("rs", 4),
                  ("hmask", 16), ("iota0", 2 * E0), ("iota1", 2 * E1), ("ecap0", E0), ("ecap1", E1),
                  ("cmp", 16), ("j", 1), ("j128", 1), ("mhalf", 1)):
    CONST[_name] = (_at, _n)
    _at += _n
NCONST = _at


def constants():
    c = np.zeros((128, NCONST), np.float32)

    def put(name, a):
        o, n = CONST[name]
        c[:, o:o + n] = np.broadcast_to(np.asarray(a, np.float32), (128, n))

    p = np.arange(128)
    put("ident", np.eye(128))
    put("triu", p[:, None] <= p[None, :])
    put("strict", p[:, None] < p[None, :])
    put("neg", np.where(p[None, :] > p[:, None], -1e30, 0.0))
    inv = np.float32(1.0) / np.float32(10000.0) ** (np.arange(0, HD0, 2, dtype=np.float32) / np.float32(HD0))
    ang = p[:, None].astype(np.float32) * inv[None, :].astype(np.float32)
    cos, sin = np.cos(ang).astype(np.float32), np.sin(ang).astype(np.float32)
    put("rc", np.repeat(cos, 2, axis=1))
    put("rs", sin)
    put("hmask", p[:, None] // HD0 == np.arange(16)[None, :])
    put("iota0", np.tile(np.arange(E0), 2))
    put("iota1", np.tile(np.arange(E1), 2))
    put("ecap0", np.arange(E0) * CAP)
    put("ecap1", np.arange(E1) * CAP)
    put("cmp", np.arange(16) * 128)
    put("j", p[:, None])
    put("mhalf", -0.5)
    put("j128", p[:, None] * 128)
    return c


class Queue:

    def __init__(self, name):
        self.name, self.ops, self.t = name, [], 0.0


class Ring:

    def __init__(self, tiles, first=()):
        self.tiles, self.left, self.free = tiles, [list(first) for _ in tiles], list(range(len(tiles)))
        self.asked, self.served = 0, 0

    def give(self, i, *tokens):
        assert i not in self.free
        self.free.append(i)
        self.left[i] = list(tokens)


class Weave:

    def __init__(self, when):
        self.when, self.live, self.age = when, [], 0

    def spawn(self, gen):
        done = []
        self.live.append([[], self.age, gen, done])
        return lambda: bool(done)

    def run(self, gens, depth, slope):
        todo, n = list(gens), 0
        while todo or self.live:
            while todo and sum(1 for e in self.live if len(e) == 5) < depth:
                self.live.append([[], n, todo.pop(0), [], True])
                n += 1
            best = None
            for e in self.live:
                if callable(e[0]):
                    if not e[0]():
                        continue
                    e[0] = []
                key = self.when(e[0]) + slope * e[1]
                if best is None or key < best[0]:
                    best = (key, e)
            assert best, "no generator can go on"
            e = best[1]
            self.age = e[1]
            want = next(e[2], "end")
            if want == "end":
                e[3].append(True)
                self.live.remove(e)
            else:
                e[0] = want if callable(want) else [want]


def program(nc, a, out):
    with ExitStack() as ctx:
        sems = {}

        def sem(name):
            if name not in sems:
                sems[name] = [ctx.enter_context(nc.semaphore(name)), 0]
            return sems[name]

        pe, dve, act, pool, sp = (Queue(n) for n in ("s_pe", "s_dve", "s_act", "s_pool", "s_sp"))

        def flat(ws):
            for w in ws:
                if w is None:
                    continue
                if isinstance(w, list) or not isinstance(w[0], str):
                    yield from flat(w)
                else:
                    yield w

        expected, line = {}, Queue("line")
        DELAY = {"s_pe": 200, "s_dve": 200, "s_act": 200, "s_pool": 200}

        def when(ws):
            return max([expected.get(w, 0.0) for w in flat(ws)], default=0.0)

        def price(q, fn):
            if not isinstance(fn, partial):
                return 100.0
            name = fn.func.__name__
            n = max(int(np.prod(v.shape[1:])) for v in (*fn.args, *fn.keywords.values()) if isinstance(v, bass.AP))
            if q is pe:
                if name == "transpose":
                    return 214.0
                n = int(np.prod(fn.args[0].shape[1:]))
                return max(n, 128) * 1.67 if fn.args[2].dtype == F32 else max(n, 64) * 0.42
            if q is dve:
                return 67 + n * 1.044
            if q is act:
                return 51 + n * 0.834 + (186 if "accum_out" in fn.keywords else 0)
            return 464.0 if ALU.pow in fn.args else 150 + n * 2.1

        def spend(q, fn, waits, ns=None):
            q.t = max(q.t, when(waits)) + (price(q, fn) if ns is None else ns)
            return q.t

        def op(q, fn, *waits, ns=None):
            s = sem(q.name)
            s[1] += 1
            q.ops.append((waits, fn, (q.name, 1)))
            expected[(q.name, s[1])] = spend(q, fn, waits, ns) + DELAY[q.name]
            return (q.name, s[1])

        def quiet(q, fn, *waits, ns=None):
            q.ops.append((waits, fn, None))
            spend(q, fn, waits, ns)

        def dma(q, name, dst, src, *waits, fn=None):
            s = sem(name)
            s[1] += 16
            q.ops.append((waits, fn or (lambda e: e.dma_start(dst, src)), (name, 16)))
            size = 4 * int(np.prod(dst.shape)) if fn is None else 4 * 128 * D
            line.t = max(line.t, spend(q, None, waits, 1040 if q is pool else 60)) + size / 250
            expected[(name, s[1])] = line.t + 2000
            return (name, s[1])

        weave = Weave(when)
        spawn = weave.spawn

        def grab(ring):
            turn = ring.asked
            ring.asked += 1
            if ring.served < turn or not ring.free:
                yield lambda: ring.served == turn and bool(ring.free)
            ring.served += 1
            i = min(ring.free, key=lambda i: when(ring.left[i]))
            ring.free.remove(i)
            yield ring.left[i]
            return i, ring.tiles[i], ring.left[i]

        def play(q, e):
            seen = {}
            for waits, fn, inc in q.ops:
                need = {}
                for name, v in flat(waits):
                    need[name] = max(need.get(name, 0), v)
                for name, v in need.items():
                    if seen.get(name, 0) < v:
                        e.wait_ge(sems[name][0], v)
                        seen[name] = v
                r = fn() if isinstance(fn, partial) else fn(e)
                if inc:
                    r.then_inc(sems[inc[0]][0], inc[1])

        def sb(name, shape, dt=F32):
            return ctx.enter_context(nc.sbuf_tensor(name, shape, dt))

        def twice(name, cols, cuts):
            with nc.sbuf_tensor(name, [128, cols], F32) as t:
                pass
            ends = [*cuts, cols]
            parts = [(lo, hi, sb(f"{name}R{lo}", [128, hi - lo], F32R)) for lo, hi in zip([0, *cuts], ends)]

            def part(lo, n):
                at, v = next((lo_, v) for lo_, hi_, v in parts if lo_ <= lo and lo + n <= hi_)
                return v[:, lo - at:lo - at + n]
            return t, part

        X = sb("X", [128, NB, D])
        CT, ctr = twice("CT", NB * D, [])
        CT = CT[:, :].rearrange("p (b k t) -> p b k t", b=NB, k=2)
        CTR = ctr(0, NB * D).rearrange("p (b k t) -> p b k t", b=NB, k=2)
        TT = [sb(f"TT{i}", [128, D]) for i in range(3)]
        BIG, bigr = twice("BIG", BIGKB * KB, [at * KB for at in (16, 24, 32, 56, 72, 80, 96, 104, 120)])
        W0, XW0, WK0 = 0, 96 * KB, 128 * KB
        CS = sb("CS", [128, NCONST])
        cst = {k: CS[:, o:o + n] for k, (o, n) in CONST.items()}
        identb = sb("identb", [128, 128], BF16)
        strictb = sb("strictb", [128, 128], BF16)
        onesb = sb("onesb", [128, 128], BF16)
        negb = sb("negb", [128, 128], BF16)
        st = sb("st", [128, 8, 16])
        zero = sb("zero", [128, D])
        v8 = sb("v8", [128, NB, 8])
        i8 = sb("i8", [128, NB, 8], U32)
        OH = sb("OH", [128, NB, 2, E1], BF16)
        CNT = sb("CNT", [128, NB + 1, E1])
        PF = sb("PF", [128, NB, 2])
        PI = sb("PI", [128, NB, 2], I32)
        YI = sb("YI", [128, NB, 2], I32)
        GW = sb("GW", [128, NB, 2])
        RT = sb("RT", [128, 4, 32])
        RC = sb("RC", [128, 8 * 32])
        TI = sb("TI", [128, 2], I32)
        sc = sb("sc", [128, 40])
        ident, ident_f = cst["ident"], cst["ident"]

        bank_t = [ctx.enter_context(nc.psum_tensor(f"ps{i}", [128, 512], F32)) for i in range(8)]
        banks = Ring(bank_t)
        XS = nc.dram_tensor("xs_dram", [E1 * CAP, D], F32, kind="Internal").ap()
        YS = nc.dram_tensor("ys_dram", [NT1 * 128, D], F32, kind="Internal").ap()

        def big(at_kb, cnt, r=False, **kw):
            v = bigr(at_kb * KB, cnt) if r else BIG[:, at_kb * KB:at_kb * KB + cnt]
            if kw:
                pat = kw.pop("pat")
                v = v.rearrange(pat, **kw)
            return v

        small = sb("small", [128, 256 + 384 + 256 + 2 * E0 + 256 + 2])
        xv = a["x"].rearrange("b p f -> p b f")
        t_x = []
        for g in range(4):
            t = dma(sp, f"d_x{g}", X[:, 4 * g:4 * g + 4, :], xv[:, 4 * g:4 * g + 4, :])
            t_x += [t] * 4
            if g == 0:
                t_cst = dma(sp, "d_cst", CS[:, :], a["consts"])
                t_ct0 = dma(sp, "d_ct0", CT[:, 0:4, :, :], a["ctxT"][:, 0:4, :, :])
                t_small = dma(sp, "d_small", small[:, :], a["small0"])
        t_ct1 = dma(sp, "d_ct1", CT[:, 4:NB, :, :], a["ctxT"][:, 4:NB, :, :])
        wdn = small[:, 0:256].rearrange("p (k n) -> p k n", k=2)
        wqkv = small[:, 256:640]
        wup = small[:, 640:896]
        rt0 = small[:, 896:912].rearrange("p (k n) -> p k n", k=2)
        g2b = small[:, 912:1168]
        g1c = small[:, 1168:1170]

        WGU0 = big(0, 64 * KB)
        WD0 = big(64, 32 * KB)
        t_w0 = [dma(sp, "d_wgu0", WGU0, a["wgu0"]), dma(sp, "d_wd0", WD0, a["wd0"])]

        t_k = [op(act, partial(nc.scalar.copy, identb[:, :], ident), t_cst),
               op(act, partial(nc.scalar.copy, strictb[:, :], cst["strict"]), t_cst),
               op(act, partial(nc.scalar.copy, negb[:, :], cst["neg"]), t_cst),
               op(dve, partial(nc.vector.memset, onesb[:, :], 1.0)),
               op(dve, partial(nc.vector.memset, zero[:, :], 0.0))]
        t_rc = op(dve, partial(nc.vector.memset, RC[:, :], 0.0))
        t_wdn = [op(act, partial(nc.scalar.mul, wdn[:, k, :], wdn[:, k, :], g1c[:, k:k + 1]), t_small)
                 for k in range(2)]

        stat = Ring([st[:, i, :] for i in range(8)])

        def rsqrt(dst, src, *ready):
            t = op(dve, partial(nc.vector.tensor_scalar, dst, src, EPS, None, ALU.add), *ready)
            yield t
            t = op(pool, partial(nc.gpsimd.tensor_tensor, dst, dst, cst["mhalf"], ALU.pow), t, t_cst)
            yield t
            return t

        def layernorm(src, dst, *ready):
            i, s, free = yield from grab(stat)
            yield list(ready)
            t = op(dve, partial(nc.vector.bn_stats, s[:, 0:6], src), list(ready), free)
            t = op(dve, partial(nc.vector.bn_aggr, s[:, 6:8], s[:, 0:6]), t)
            t = yield from rsqrt(s[:, 8:9], s[:, 7:8], t)
            t = op(dve, partial(nc.vector.tensor_scalar, dst, src, s[:, 6:7], s[:, 8:9], ALU.subtract, ALU.mult), t)
            stat.give(i, t)
            yield t
            return t

        def twice_normal(src, *ready):
            i, s, free = yield from grab(stat)
            yield list(ready)
            t = op(dve, partial(nc.vector.bn_stats, s[:, 0:6], src), list(ready), free)
            t = op(dve, partial(nc.vector.bn_aggr, s[:, 6:8], s[:, 0:6]), t)
            t1 = op(dve, partial(nc.vector.tensor_scalar, s[:, 8:9], s[:, 7:8], EPS, None, ALU.add), t)
            t2 = op(dve, partial(nc.vector.tensor_scalar, s[:, 9:10], s[:, 7:8], 1.0 + EPS, EPS * EPS, ALU.mult, ALU.add), t)
            yield t1, t2
            t = op(pool, partial(nc.gpsimd.tensor_tensor, s[:, 8:10], s[:, 8:10],
                                 cst["mhalf"].broadcast_to([128, 2]), ALU.pow), t1, t2, t_cst)
            yield t
            return i, s, t

        def transposes(src, n, *ready):
            yield list(ready)
            i, bk, free = yield from grab(banks)
            for k in range(n):
                f = partial(nc.tensor.transpose, bk[:, k * 128:(k + 1) * 128], src[:, k * 128:(k + 1) * 128], ident)
                if k < n - 1:
                    quiet(pe, f, list(ready), free, t_cst)
                else:
                    t = op(pe, f, list(ready), free, t_cst)
            yield t
            return i, bk, t

        def mm(o, l, r, start, stop, last, *waits):
            f = partial(nc.tensor.matmul, o, l, r, start=start, stop=stop)
            if last:
                return op(pe, f, *waits)
            quiet(pe, f, *waits)

        def mm3(o, l, r, start, stop, last, *waits):
            t = None
            for n, (i, j) in enumerate(((0, 0), (0, 1), (1, 0))):
                f = partial(nc.tensor.matmul, o, l[i], r[j],
                            start=start and n == 0, stop=stop and n == 2)
                if last and n == 2:
                    t = op(pe, f, *waits)
                else:
                    quiet(pe, f, *waits)
            return t

        def high(dst, src, *waits):
            return op(act, partial(nc.scalar.copy, dst, src), *waits)

        def low(dst, src, hi, *waits):
            return op(dve, partial(nc.vector.tensor_tensor, dst, src, hi.bitcast(F32), ALU.subtract), *waits)

        def evac(q, dst, src, *waits):
            if q is act:
                return op(act, partial(nc.scalar.copy, dst, src), *waits)
            return op(dve, partial(nc.vector.tensor_copy, dst, src), *waits)

        class Route:
            pass

        def route_tile(R, b, logits_bank, t_log, itt, tt, t_tt):
            E, bi, bk = R.E, *logits_bank
            il, lg, f = yield from grab(R.rt)
            lg = lg[:, 0:E]
            yield t_log
            t = op(dve, partial(nc.vector.tensor_copy, lg, bk[:, 0:E]), t_log, f)
            banks.give(bi, t)
            t1 = op(dve, partial(nc.vector.max, v8[:, b, :], lg), t, R.v8free)
            t2 = op(dve, partial(nc.vector.max_index, i8[:, b, :], v8[:, b, :], lg), t1, R.v8free)
            R.v8.append(t2)
            oh = OH[:, b, :, 0:E]
            t_oh = op(dve, partial(nc.vector.tensor_tensor, oh, cst[R.iota].rearrange("p (k n) -> p k n", k=2),
                                   i8[:, b, 0:2].rearrange("p (k o) -> p k o", o=1).broadcast_to([128, 2, E]),
                                   ALU.is_equal), t2, R.ohfree)
            im, m, f = yield from grab(R.mb)
            m = m[:, 0:E]
            t_m = op(dve, partial(nc.vector.tensor_tensor, m, oh[:, 0, :], oh[:, 1, :], ALU.add), t_oh, f)
            yield t_m
            pi_, pb, free = yield from grab(banks)
            mm(pb[:, 0:E], strictb[:, :], m, True, True, False, t_m, free, t_k)
            t_r = mm(pb[:, E:2 * E], onesb[:, :], m, True, True, True)
            R.mb.give(im, t_r)
            ir, pr, f = yield from grab(R.pr)
            pr = pr[:, 0:2 * E].rearrange("p (k n) -> p k n", k=2)
            yield t_r
            n = R.n
            R.n += 1
            t_p = op(dve, partial(nc.vector.tensor_tensor, lg, pb[:, 0:E], CNT[:, n, 0:E], ALU.add), t_r, t2, R.cnt)
            R.cnt = op(dve, partial(nc.vector.tensor_tensor, CNT[:, n + 1, 0:E], pb[:, E:2 * E], CNT[:, n, 0:E], ALU.add),
                       t_r, R.cnt)
            banks.give(pi_, R.cnt)
            t_q = op(dve, partial(nc.vector.tensor_tensor, pr, oh, lg.rearrange("p (o n) -> p o n", o=1)
                                  .broadcast_to([128, 2, E]), ALU.mult), t_p, f)
            R.rt.give(il, t_q)
            t_f = op(dve, partial(nc.vector.tensor_reduce, PF[:, b, :], pr, AX, ALU.add), t_q, R.pffree)
            R.pr.give(ir, t_f)
            t_i = op(dve, partial(nc.vector.tensor_copy, PI[:, b, :], PF[:, b, :]), t_f, R.pifree)
            R.pf.append(t_f)
            yield t_i
            for k in range(2):
                t = dma(pool, f"d_sc{itt}", None, None, t_i, t_tt, R.xsfree, t_k,
                        fn=partial(nc.gpsimd.indirect_dma_start, XS,
                                   bass.IndirectOffsetOnAxis(ap=PI[:, b, k:k + 1], axis=0), tt[:, :], None))
            R.scat.append(t)
            return t

        def route_start(E, names, prev):
            R = Route()
            R.E, R.NT, R.n = E, 32 + E - 1, 0
            R.iota, R.ecap = names
            R.rt = Ring([RT[:, i, :] for i in range(4)], [prev])
            R.mb = Ring([m[:, :] for m in mb0], [prev])
            R.pr = Ring([pr0[:, i, :] for i in range(2)], [prev])
            R.pf, R.scat, R.v8 = [], [], []
            R.v8free = R.pffree = R.ohfree = R.pifree = R.xsfree = prev
            R.cnt = op(dve, partial(nc.vector.tensor_copy, CNT[:, 0, 0:E], cst[R.ecap]), t_cst, prev)
            return R

        def route_end(R, queues):
            E = R.E
            t_pad = op(dve, partial(nc.vector.tensor_copy, R.pad, CNT[:, NB, 0:E]), R.cnt)
            for x in range(E):
                def pad(e, x=x):
                    v = e.value_load(R.pad[0:1, x:x + 1], min_val=0, max_val=E * CAP - 128)
                    return e.dma_start(XS[bass.ds(v, 128), :], zero[:, :])
                dma(queues[x % 2], f"d_pad{x % 2}", None, None, t_pad, t_k, R.xsfree, fn=pad)
            R.tpad = [(f"d_pad{i}", sem(f"d_pad{i}")[1]) for i in range(2)]
            RC3 = R.ohw.rearrange("p a n -> p (a n)")[:, 0:E * 16].rearrange("p (n j) -> p n j", n=E)
            buf = [RC[:, 32 * i:32 * i + 32] for i in range(6)]
            nn, nt, of, w1 = sc[:, 0:E], sc[:, 16:16 + E], RC[:, 192:192 + E], RC[:, 224:224 + E]
            t = op(dve, partial(nc.vector.tensor_tensor, nn, CNT[:, NB, 0:E], cst[R.ecap], ALU.subtract), R.cnt, R.scfree)
            t = op(dve, partial(nc.vector.tensor_tensor, RC3, nn.rearrange("p (n o) -> p n o", o=1)
                                                  .broadcast_to([128, E, 16]),
                                                  cst["cmp"].rearrange("p (o j) -> p o j", o=1)
                                                  .broadcast_to([128, E, 16]), ALU.is_gt),
                   t, t_rc, R.tifree, R.ohwfree)
            t = t_cmp = op(dve, partial(nc.vector.tensor_reduce, nt, RC3, AX, ALU.add), t)
            t_nt = t
            t = op(dve, partial(nc.vector.tensor_copy, buf[0][:, 16:16 + E], nt), t)
            k, i = 1, 0
            while k < E:
                t = op(dve, partial(nc.vector.tensor_tensor, buf[i + 1][:, 16:16 + E], buf[i][:, 16:16 + E],
                                                                buf[i][:, 16 - k:16 - k + E], ALU.add), t)
                k, i = 2 * k, i + 1
            inc = buf[i][:, 16:16 + E]
            t_of = op(dve, partial(nc.vector.tensor_tensor, of, nt, inc, ALU.subtract), t, t_nt)
            t_of = op(dve, partial(nc.vector.scalar_tensor_tensor, out=of, in0=of, scalar=128.0, in1=cst[R.ecap],
                                                            op0=ALU.mult, op1=ALU.add), t_of)
            t = op(dve, partial(nc.vector.tensor_scalar, w1, inc, cst["j"], None, ALU.is_le), t)
            te, va, r = sc[:, 32:33], sc[:, 33:34], sc[:, 34:35]
            t = op(dve, partial(nc.vector.tensor_reduce, te, w1, AX, ALU.add), t)
            t_va = op(dve, partial(nc.vector.tensor_scalar, va, te, float(E), None, ALU.is_lt), t)
            t = op(dve, partial(nc.vector.tensor_tensor, te, te, va, ALU.mult), t_va)
            t_te = t
            t = op(dve, partial(nc.vector.tensor_scalar, w1, cst[R.iota][:, 0:E], te, None, ALU.is_equal), t)
            t = op(dve, partial(nc.vector.tensor_tensor, w1, w1, of, ALU.mult), t, t_of)
            t = op(dve, partial(nc.vector.tensor_reduce, r, w1, AX, ALU.add), t)
            t = op(dve, partial(nc.vector.tensor_scalar, r, r, cst["j128"], va, ALU.add, ALU.mult), t, t_va)
            t1 = op(dve, partial(nc.vector.tensor_copy, TI[:, 0:1], te), t_te, R.tifree)
            R.ti = op(dve, partial(nc.vector.tensor_copy, TI[:, 1:2], r), t, R.tifree)
            OHw = R.ohw
            oh = OH[:, :, :, 0:E].rearrange("p b k n -> p (b k) n")
            t = op(dve, partial(nc.vector.tensor_tensor, OHw, oh, of.rearrange("p (o n) -> p o n", o=1)
                                                  .broadcast_to([128, 2 * NB, E]), ALU.mult), t_of, t_cmp, R.ohwfree)
            y1 = R.y1
            t = op(dve, partial(nc.vector.tensor_reduce, y1, OHw, AX, ALU.add), t)
            t = op(dve, partial(nc.vector.tensor_tensor, y1, PF[:, :, :].rearrange("p b k -> p (b k)"), y1, ALU.subtract),
                   t, R.pf)
            R.yi = op(dve, partial(nc.vector.tensor_copy, YI[:, :, :].rearrange("p b k -> p (b k)"), y1), t, R.yifree)

        mb0 = [sb(f"mb{i}", [128, E1], BF16) for i in range(2)]
        pr0 = sb("pr0", [128, 2, 32])

        RS = 96
        def space(*spans):
            spans = [[lo * KB, hi * KB] for lo, hi in spans]

            def ring(n, cols, first=(), r=False):
                tiles = []
                for _ in range(n):
                    s = next(s for s in spans if s[0] + cols <= s[1])
                    tiles.append(bigr(s[0], cols) if r else BIG[:, s[0]:s[0] + cols])
                    s[0] += cols
                return Ring(tiles, first)
            return ring

        ring = space((96, BIGKB))
        r_h = ring(6, D)
        r_v0 = ring(4, 16 * 9)
        r_qkT = ring(4, 256)
        r_o = ring(4, 128)
        r_rs = ring(6, 8)
        for i, v in enumerate(r_v0.tiles):
            ones = v.rearrange("p (h d) -> p h d", d=9)[:, :, 8:9]
            r_v0.left[i] = [op(dve, partial(nc.vector.memset, ones, 1.0))]
        r_q0 = ring(2, D)
        r_a = ring(2, 128)
        r_hn = ring(2, D)
        r_hnT = ring(3, D)
        r_tT = r_hnT
        r_cT = ring(2, 128)
        r_qk = ring(2, 256)
        r_m = ring(2, 256)
        r_oT = ring(2, 128)
        r_r = ring(2, D)
        r_sq = ring(1, D)
        r_km = ring(3, 512)
        r_p = ring(4, 512)
        r_pt = ring(4, 512)
        r_sm = ring(8, 16)
        r_tt = Ring(TT)
        PADI = sb("PADI", [128, E1], I32)
        Y1 = sb("Y1", [128, 2 * NB])
        KMACT = 1
        SC0 = float(np.float32(1.0) / np.sqrt(np.float32(HD0)))

        R0 = route_start(E0, ("iota0", "ecap0"), None)
        R0.scfree = None
        R0.pad, R0.y1, R0.tifree, R0.ohwfree, R0.yifree = PADI[:, 0:E0], Y1[:, :], None, None, None
        res_done = {}

        def latent_tile(b):
            x = X[:, b, :]
            tct = t_ct0 if b < 4 else t_ct1
            iq, q0, f = yield from grab(r_q0)
            t_q0 = yield from layernorm(x, q0, t_x[b], f)
            ia, A, f_a = yield from grab(r_a)
            yield tct
            bi, bk, f = yield from grab(banks)
            for k in range(2):
                t = mm(bk[:, 0:128], CT[:, b, k, :], CT[:, b, k, :], k == 0, k == 1, k == 1, tct, f)
            yield t
            t_a = op(dve, partial(nc.vector.tensor_tensor, A, bk[:, 0:128], cst["triu"], ALU.mult), t, f_a, t_cst)
            banks.give(bi, t_a)
            t_a = op(dve, partial(nc.vector.tensor_tensor, A, A, ident, ALU.add), t_a)
            yield t_a
            bi, bk, f = yield from grab(banks)
            t = mm(bk[:, 0:D], A, q0, True, True, True, t_a, t_q0, f)
            r_a.give(ia, t)
            r_q0.give(iq, t)
            yield t
            t_x1 = op(dve, partial(nc.vector.tensor_tensor, x, bk[:, 0:D], x, ALU.add), t, t_q0)
            banks.give(bi, t_x1)
            ih, h, f = yield from grab(r_h)
            i_s, sx, t = yield from twice_normal(x, t_x1)
            ihn, hn, f2 = yield from grab(r_hn)
            t_hn = op(dve, partial(nc.vector.tensor_scalar, hn, x, sx[:, 6:7], sx[:, 9:10], ALU.subtract, ALU.mult), t, f2)
            t_h = op(dve, partial(nc.vector.tensor_scalar, h, x, sx[:, 6:7], sx[:, 8:9], ALU.subtract, ALU.mult), t, f)
            stat.give(i_s, t_hn, t_h)
            iT, hnT, f = yield from grab(r_hnT)
            bi, bk, t = yield from transposes(hn, 2, t_hn)
            r_hn.give(ihn, t)
            t_hnT = evac(act, hnT, bk[:, 0:D], t, f)
            banks.give(bi, t_hnT)
            ic, cT, f_c = yield from grab(r_cT)
            yield t_hnT
            bi, bk, f = yield from grab(banks)
            for k in range(2):
                t = mm(bk[:, 0:128], wdn[:, k, :], hnT[:, k * 128:(k + 1) * 128], k == 0, k == 1, k == 1,
                       t_hnT, t_wdn, f)
            r_hnT.give(iT, t)
            yield t
            t_cT = evac(act, cT, bk[:, 0:128], t, f_c)
            banks.give(bi, t_cT)
            iv, v, f_v = yield from grab(r_v0)
            ik, qkT, f_k = yield from grab(r_qkT)
            io, o_, f_o = yield from grab(r_o)
            iqk, qk, f_q = yield from grab(r_qk)
            im, m, f_m = yield from grab(r_m)
            yield t_cT
            bi, bk, f = yield from grab(banks)
            t = mm(bk[:, 0:384], cT, wqkv, True, True, True, t_cT, t_small, f)
            r_cT.give(ic, t)
            yield t
            t_v = evac(act, v.rearrange("p (h d) -> p h d", d=9)[:, :, 0:8],
                       bk[:, 256:384].rearrange("p (h d) -> p h d", d=8), t, f_v)
            t_qk = evac(act, qk, bk[:, 0:256], t, f_q)
            banks.give(bi, t_qk)
            yield t_qk
            rsb = cst["rs"].rearrange("p (o n) -> p o n", o=1).broadcast_to([128, 32, 4])
            rcb = cst["rc"].rearrange("p (o n) -> p o n", o=1).broadcast_to([128, 32, 8])
            q8 = qk.rearrange("p (h n) -> p h n", h=32)
            qv = qk.rearrange("p (h n two) -> p h n two", h=32, two=2)
            mv = m.rearrange("p (h n two) -> p h n two", h=32, two=2)
            t2 = op(pool, partial(nc.gpsimd.tensor_tensor, mv[:, :, :, 0], qv[:, :, :, 1], rsb, ALU.mult), t_qk, f_m, t_cst)
            t3 = op(pool, partial(nc.gpsimd.tensor_tensor, mv[:, :, :, 1], qv[:, :, :, 0], rsb, ALU.mult), t_qk, f_m)
            t1 = op(pool, partial(nc.gpsimd.tensor_tensor, q8, q8, rcb, ALU.mult), t2, t3)
            yield t1
            q2 = qk.rearrange("p (n two) -> p n two", two=2)
            m2 = m.rearrange("p (n two) -> p n two", two=2)
            t4 = op(dve, partial(nc.vector.tensor_tensor, q2[:, :, 0], q2[:, :, 0], m2[:, :, 0], ALU.subtract), t1)
            t5 = op(dve, partial(nc.vector.tensor_tensor, q2[:, :, 1], q2[:, :, 1], m2[:, :, 1], ALU.add), t1)
            r_m.give(im, t4, t5)
            bi, bk, t = yield from transposes(qk, 2, t4, t5)
            r_qk.give(iqk, t)
            t_qkT = evac(act, qkT, bk[:, 0:256], t, f_k)
            banks.give(bi, t_qkT)
            yield t_qkT
            t_o, used = [], []
            for k in [spawn(latent_heads(g, qkT, t_qkT, v, t_v, o_, f_o, t_o, used)) for g in range(4)]:
                yield k
            r_v0.give(iv, used)
            r_qkT.give(ik, used)
            iT, oT, f_t = yield from grab(r_oT)
            bi, bk, t = yield from transposes(o_, 1, t_o)
            r_o.give(io, t)
            t_oT = evac(act, oT, bk[:, 0:128], t, f_t)
            banks.give(bi, t_oT)
            ir, r, f_r = yield from grab(r_r)
            yield t_oT
            bi, bk, f = yield from grab(banks)
            t = mm(bk[:, 0:D], oT, wup, True, True, True, t_oT, t_small, f)
            r_oT.give(iT, t)
            yield t
            t_r = op(dve, partial(nc.vector.tensor_tensor, r, bk[:, 0:D], h, ALU.add), t, t_h, f_r)
            banks.give(bi, t_r)
            r_h.give(ih, t_r)
            isq, sq, f = yield from grab(r_sq)
            irs, rs, f_rs = yield from grab(r_rs)
            yield t_r
            t = op(act, partial(nc.scalar.activation, sq, r, ACT.Square, scale=1.0 / 16, accum_out=rs[:, 2:3]), t_r, f, f_rs)
            r_sq.give(isq, t)
            yield t
            t = yield from rsqrt(rs[:, 3:4], rs[:, 2:3], t)
            itt, tt, f = yield from grab(r_tt)
            t_tt = op(dve, partial(nc.vector.scalar_tensor_tensor, out=tt[:, :], in0=r, scalar=rs[:, 3:4], in1=g2b,
                                   op0=ALU.mult, op1=ALU.mult), t, t_small, f)
            r_rs.give(irs, t_tt)
            t_xr = (op(dve, partial(nc.vector.tensor_tensor, x, x, r, ALU.add), t_r, t_h) if b >= 12 else
                    op(pool, partial(nc.gpsimd.tensor_tensor, x, x, r, ALU.add), t_r, t_h))
            r_r.give(ir, t_tt, t_xr)
            res_done[b] = t_xr
            iT, tT, f = yield from grab(r_tT)
            bi, bk, t = yield from transposes(tt, 2, t_tt)
            t_tT = evac(act, tT, bk[:, 0:D], t, f)
            t_ttpe = t
            banks.give(bi, t_tT)
            yield t_tT
            bi, bk, f = yield from grab(banks)
            for k in range(2):
                t = mm(bk[:, 0:E0], tT[:, k * 128:(k + 1) * 128], rt0[:, k, :], k == 0, k == 1, k == 1,
                       t_tT, t_small, f)
            r_tT.give(iT, t)
            t_sc = yield from route_tile(R0, b, (bi, bk), t, itt, tt, t_tt)
            r_tt.give(itt, t_sc, t_ttpe)

        def latent_heads(g, qkT, t_qkT, v, t_v, o_, f_o, t_o, used):
            kTb = qkT[:, 128:256].rearrange("p (o n) -> p o n", o=1).broadcast_to([128, 4, 128])
            ikm, km, f = yield from grab(r_km)
            hm = cst["hmask"][:, 4 * g:4 * g + 4].rearrange("p (n o) -> p n o", o=1).broadcast_to([128, 4, 128])
            if g < KMACT:
                for n in range(4):
                    t_km = op(act, partial(nc.scalar.mul, km[:, n * 128:(n + 1) * 128], qkT[:, 128:256],
                                           cst["hmask"][:, 4 * g + n:4 * g + n + 1]), t_qkT, f)
            else:
                t_km = op(dve, partial(nc.vector.tensor_tensor, km.rearrange("p (n t) -> p n t", n=4), kTb, hm, ALU.mult),
                          t_qkT, f)
            ism, sm, f_sm = yield from grab(r_sm)
            ip, p, f_p = yield from grab(r_p)
            yield t_km
            bi, bk, f = yield from grab(banks)
            mm(bk[:, :].rearrange("p (n t) -> p n t", n=4), identb[:, :],
               negb[:, :].rearrange("p (o t) -> p o t", o=1).broadcast_to([128, 4, 128]), True, False, False, f, t_k)
            t_s = mm(bk[:, :], qkT[:, 0:128], km, False, True, True, t_km, t_qkT)
            r_km.give(ikm, t_s)
            used += [t_s, t_km]
            yield t_s
            t = op(dve, partial(nc.vector.tensor_reduce, sm[:, 0:4], bk[:, :].rearrange("p (n t) -> p n t", n=4), AX,
                                ALU.max), t_s, f_sm)
            t_nm = op(dve, partial(nc.vector.tensor_scalar, sm[:, 4:8], sm[:, 0:4], -SC0, None, ALU.mult), t)
            yield t_nm
            for n in range(4):
                t_e = op(act, partial(nc.scalar.activation, p[:, n * 128:(n + 1) * 128], bk[:, n * 128:(n + 1) * 128],
                                      ACT.Exp, bias=sm[:, 4 + n:5 + n], scale=SC0), t_nm, f_p)
            banks.give(bi, t_e)
            ipt, pt, f = yield from grab(r_pt)
            yield t_e
            bi, bk, t = yield from transposes(p, 4, t_e)
            r_p.give(ip, t)
            t_pt = evac(act, pt, bk[:, :], t, f)
            banks.give(bi, t_pt)
            yield t_pt
            bi, bk, f = yield from grab(banks)
            for n in range(4):
                hh = 4 * g + n
                t = mm(bk[:, n * 9:n * 9 + 9], pt[:, n * 128:(n + 1) * 128],
                       v[:, hh * 9:hh * 9 + 9], True, True, n == 3, t_pt, t_v, f)
            used.append(t)
            r_pt.give(ipt, t)
            yield t
            og = o_[:, 32 * g:32 * g + 32].rearrange("p (n d) -> p n d", n=4)
            pv = bk[:, 0:36].rearrange("p (n d) -> p n d", n=4)
            sums = sm[:, 8:12].rearrange("p (n o) -> p n o", o=1)
            t_r = op(dve, partial(nc.vector.reciprocal, sums, pv[:, :, 8:9]), t)
            t = op(dve, partial(nc.vector.tensor_tensor, og, pv[:, :, 0:8], sums.broadcast_to([128, 4, 8]), ALU.mult),
                   t_r, f_o)
            banks.give(bi, t)
            r_sm.give(ism, t)
            t_o.append(t)

        weave.run((latent_tile(b) for b in range(NB)), 10, 100.0)

        def now():
            return [(n, sem(n)[1]) for n in ("s_pe", "s_dve", "s_act", "s_pool")]

        R0.ohw = big(152, 2 * NB * E0, pat="p (a n) -> p a n", n=E0)
        R0.ohwfree = now()
        route_end(R0, (sp, act))

        def gates(R, sigmoid):
            g = GW[:, :, :]
            if sigmoid:
                t = op(act, partial(nc.scalar.activation, g, v8[:, :, 0:2], ACT.Exp, scale=-1.0), R.v8, R.gwfree)
                t = op(dve, partial(nc.vector.tensor_scalar, g, g, 1.0, None, ALU.add), t)
                return op(dve, partial(nc.vector.reciprocal, g, g), t)
            t = op(dve, partial(nc.vector.tensor_tensor, GW[:, :, 1], v8[:, :, 1], v8[:, :, 0], ALU.subtract), R.v8)
            t = op(act, partial(nc.scalar.activation, GW[:, :, 1], GW[:, :, 1], ACT.Exp), t)
            t = op(dve, partial(nc.vector.tensor_scalar, GW[:, :, 0], GW[:, :, 1], 1.0, None, ALU.add), t)
            t = op(dve, partial(nc.vector.reciprocal, GW[:, :, 0], GW[:, :, 0]), t)
            return op(dve, partial(nc.vector.tensor_tensor, GW[:, :, 1], GW[:, :, 1], GW[:, :, 0], ALU.mult), t)

        R0.gwfree = None
        R0.gw = gates(R0, False)
        end0 = now()

        WQ = big(96, 8 * KB, pat="p (k n) -> p k n", k=2)
        WKV = big(104, 16 * KB, pat="p (k n) -> p k n", k=2)
        WO = big(72, 8 * KB, pat="p (c n) -> p c n", c=8)
        small1 = sb("small1", [128, 2 + 2 + 256 + 1 + 32])
        gam, bet, bo, gt = small1[:, 0:2], small1[:, 2:4], small1[:, 4:260], small1[:, 260:261]
        rt1 = small1[:, 261:293].rearrange("p (k n) -> p k n", k=2)
        loaded = {}

        def load_attention():
            loaded["wkv"] = dma(sp, "d_wkv", big(104, 16 * KB), a["wkv1"], end0)
            loaded["s1"] = dma(sp, "d_s1", small1[:, :], a["small1"])

        def load_projections():
            loaded["wq"] = dma(sp, "d_wq", big(96, 8 * KB), a["wq1"], end1)
            loaded["wo"] = dma(sp, "d_wo", big(72, 8 * KB), a["wo1"], end1)

        def experts(R, rings, wgu, wdn_, F, t_w, t_wd2, done, others=(), also=lambda: None):
            r_w, r_wd, r_xs, r_xT, r_h, r_hT, r_y = rings
            E, K2, n = R.E, F // 128, 2 * F

            held = {}

            def expert_of(e, j):
                if (e.engine, j) not in held:
                    held[e.engine, j] = e.value_load(TI[j:j + 1, 0:1], min_val=0, max_val=E - 1)
                return held[e.engine, j]

            def down_parts(j, down):
                iD, wd, f = yield from grab(r_wd)

                def expert(e):
                    return wdn_[:, bass.ds(expert_of(e, j) * n, n)]
                yield R.ti, t_wd2, f
                t = op(act, lambda e: e.copy(wd[:, 0:n], expert(e)), R.ti, t_wd2, f, ns=51 + n * 0.834)
                yield t
                t = op(dve, lambda e: e.tensor_tensor(wd[:, n:2 * n], expert(e), wd[:, 0:n].bitcast(F32), ALU.subtract),
                       t, R.ti, t_wd2, ns=67 + n * 1.044)
                down += [iD, wd, t]

            def tile(j):
                ixs, xs, f = yield from grab(r_xs)

                def load(e):
                    v = e.value_load(TI[j:j + 1, 1:2], min_val=0, max_val=E * CAP - 128)
                    return e.dma_start(xs, XS[bass.ds(v, 128), :])
                t = dma(sp, f"d_xs{ixs}", None, None, R.ti, R.scat, R.tpad, f, fn=load)
                if j == 6:
                    also()
                iw, wt, f = yield from grab(r_w)
                yield R.ti, t_w, f
                t_wt = []
                for q, k in ((dve, 0), (act, 1)):
                    def copy(e, k=k):
                        r = expert_of(e, j)
                        put = e.tensor_copy if k == 0 else e.copy
                        return put(wt[:, k * n:(k + 1) * n], wgu[:, bass.ds(r * (2 * n) + k * n, n)])
                    t_wt.append(op(q, copy, R.ti, t_w, f, ns=60 + n * 1.04))
                down = []
                parts_done = spawn(down_parts(j, down))
                iT, xT, f = yield from grab(r_xT)
                bi, bk, t = yield from transposes(xs, 2, t)
                r_xs.give(ixs, t)
                t_xT = evac(act, xT, bk[:, 0:D], t, f)
                banks.give(bi, t_xT)
                ih, h, f_h = yield from grab(r_h)
                yield t_xT, t_wt
                ig, gk, f1 = yield from grab(banks)
                iu, uk, f2 = yield from grab(banks)
                for o_, at, fb in ((gk, 0, f1), (uk, F, f2)):
                    for c in range(K2):
                        for k in range(2):
                            w = wt[:, k * n + at + c * 128:k * n + at + (c + 1) * 128]
                            t = mm(o_[:, c * 128:(c + 1) * 128], w, xT[:, k * 128:(k + 1) * 128], k == 0, k == 1,
                                   c == K2 - 1 and k == 1, t_xT, t_wt, fb)
                    if o_ is gk:
                        t_g = t
                r_xT.give(iT, t)
                r_w.give(iw, t)
                t_u = t
                yield t_g
                t_sg = op(act, partial(nc.scalar.activation, h, gk[:, 0:F], ACT.Silu), t_g, f_h)
                banks.give(ig, t_sg)
                yield t_u, t_sg
                t_h = op(dve, partial(nc.vector.tensor_tensor, h, uk[:, 0:F], h, ALU.mult), t_u, t_sg)
                banks.give(iu, t_h)
                iH, hT, f = yield from grab(r_hT)
                yield t_h
                t_hh = high(hT[:, 0:F], h, t_h, f)
                yield t_hh
                t_hT = low(hT[:, F:2 * F], h, hT[:, 0:F], t_hh)
                r_h.give(ih, t_hT)
                iy, y, f_y = yield from grab(r_y)
                yield parts_done
                iD, wd, t_wd = down
                yield t_hT, t_wd
                bi, bk, f = yield from grab(banks)
                for k in range(K2):
                    t = mm3(bk[:, 0:D], [hT[:, i * F + k * 128:i * F + (k + 1) * 128] for i in range(2)],
                            [wd[:, i * n + k * D:i * n + (k + 1) * D] for i in range(2)],
                            k == 0, k == K2 - 1, k == K2 - 1, t_hT, t_wd, f)
                r_hT.give(iH, t)
                r_wd.give(iD, t)
                yield t
                t_y = evac(dve, y, bk[:, 0:D], t, f_y)
                banks.give(bi, t_y)
                yield t_y
                t = dma(sp, f"d_y{iy}", YS[j * 128:(j + 1) * 128, :], y, t_y, R.ysfree)
                r_y.give(iy, t)
                done[iy] = t

            weave.run([*others] + [tile(j) for j in range(R.NT)], 8, 100.0)

        ring = space((120, BIGKB))
        rings0 = [ring(2, 4 * F0, end0), space((96, 104))(1, 4 * F0, end0, r=True), ring(3, D, end0), ring(2, D, end0),
                  ring(2, F0, end0), ring(1, 2 * F0, end0, r=True), ring(3, D, end0)]
        R0.ysfree = None
        done0 = {}
        experts(R0, rings0, WGU0, WD0, F0, t_w0, t_w0, done0, also=load_attention)
        ys0 = list(done0.values())
        end1 = now()
        load_projections()
        t_wq, t_wkv, t_wo, t_s1 = (loaded[k] for k in ("wq", "wkv", "wo", "s1"))
        xs0 = [(f"d_xs{i}", sem(f"d_xs{i}")[1]) for i in range(4)]

        WGU1, WD1 = big(0, 64 * KB), big(64, 32 * KB)
        t_w1, t_wd1, t_ws, kv_done = [], [], [], []

        tg = sb("tg", [128, 1])
        btg = sb("btg", [128, D])
        t_tg = op(act, partial(nc.scalar.activation, tg[:, :], gt, ACT.Tanh), t_s1)
        t_btg = op(dve, partial(nc.vector.tensor_scalar, btg[:, :], bo, tg[:, 0:1], None, ALU.mult), t_tg, t_s1)

        G = [None]

        def gathered(R, b, ys):
            ig, g, f = yield from grab(G[0])
            g = g.rearrange("p (k n) -> p k n", k=2)
            yield R.yi, ys
            for k in range(2):
                t_g = dma(pool, f"d_g{ig}", None, None, R.yi, ys, f,
                          fn=partial(nc.gpsimd.indirect_dma_start, g[:, k, :], None, YS[0:R.NT * 128, :],
                                     bass.IndirectOffsetOnAxis(ap=YI[:, b, k:k + 1], axis=0)))
            yield t_g
            return ig, g, t_g

        def combine(R, b, got, *ready):
            ig, g, t_g = got
            x = X[:, b, :]
            t = op(dve, partial(nc.vector.scalar_tensor_tensor, out=x, in0=g[:, 0, :], scalar=GW[:, b, 0:1], in1=x,
                                                         op0=ALU.mult, op1=ALU.add), t_g, R.gw, *ready)
            t = op(dve, partial(nc.vector.scalar_tensor_tensor, out=x, in0=g[:, 1, :], scalar=GW[:, b, 1:2], in1=x,
                                                         op0=ALU.mult, op1=ALU.add), t)
            G[0].give(ig, t)
            return t

        wk_free = [end1, ys0]
        WKV2 = [big(at, 16 * KB, r=True, pat="p (k n) -> p k n", k=2) for at in (0, 104)]
        WQ2 = [big(at, 8 * KB, r=True, pat="p (k n) -> p k n", k=2) for at in (16, 96)]
        WO2 = [big(at, 8 * KB, r=True, pat="p (c n) -> p c n", c=8) for at in (24, 72)]

        def parts(w, raw, lo, hi, t_w):
            hi_, lo_ = (x[:, :, lo:hi] for x in w)
            t = high(hi_, raw[:, :, lo:hi], t_w, end1)
            yield t
            return low(lo_, raw[:, :, lo:hi], hi_, t)

        ring2 = space((32, 56))
        r_ch = ring2(2, 512, [end1], r=True)
        r_aT = ring2(2, 1024, wk_free, r=True)
        r_xnT = ring2(3, 1024, wk_free, r=True)
        ring2 = space((56, 72), (80, 96), (120, BIGKB))
        r_kT = ring2(3, 1024, [end1])
        r_v = ring2(7, 512, [end1])
        r_qT = ring2(3, 1024, wk_free)
        r_p1 = ring2(4, 512, wk_free)
        G[0] = ring2(2, 512, wk_free)
        r_pt1 = ring2(4, 512, wk_free)
        r_xn = ring2(2, D, wk_free)
        r_xf = ring2(2, D, wk_free)
        sm1 = sb("sm1", [128, 8, 16])
        r_sm1 = Ring([sm1[:, i, :] for i in range(8)])
        SC1 = float(HD1 ** -0.5)
        R1 = route_start(E1, ("iota1", "ecap1"), [end1, R0.gw, R0.yi, R0.scat, R0.tpad, xs0])
        R1.scfree = None
        t_hT, t_log1, q_free = {}, {}, []
        x4 = {}

        KS, VS, XT, normal = {}, {}, {}, set()

        t_C, t_kw, t_vw, t_qw, t_ow = {}, {}, {}, {}, []

        def weights():
            for u in range(2):
                t_kw[u] = yield from parts(WKV2, WKV, u * 512, u * 512 + 512, t_wkv)
                t_vw[u] = yield from parts(WKV2, WKV, 1024 + u * 512, 1536 + u * 512, t_wkv)
            yield t_wq
            t_qw[0] = yield from parts(WQ2, WQ, 0, 512, t_wq)
            yield lambda: 1 in normal
            yield t_wo, t_qw[0]
            t_qw[1] = yield from parts(WQ2, WQ, 512, 1024, t_wq)
            t_ow.append((yield from parts(WO2, WO, 0, D, t_wo)))

        C2, reads, units, queries = {}, {}, [], []

        def context_read(j, t):
            kv_done.append(t)
            reads.setdefault(j, []).append(t)
            if len(reads[j]) == 6:
                r_ch.give(C2[j][0], reads[j])
            if len(kv_done) == 3 * NB:
                t_w1.append(dma(sp, "d_wgu1a", big(0, 16 * KB), a["wgu1"][:, 0:16 * KB], kv_done))
                t_ws.append(dma(sp, "d_wsg", big(104, 8 * KB), a["wsgu"], kv_done))
                t_ws.append(dma(sp, "d_wsd", big(112, 4 * KB), a["wsd"], kv_done))
                r_xh.left[:] = [kv_done] * 2

        def keys(j, u):
            if u == 0:
                c = CT[:, 2 * j:2 * j + 2, :, :]
                ic, ch, f = yield from grab(r_ch)
                ch = ch.rearrange("p (b k t) -> p b k t", b=2, k=2)
                t = high(ch, c, f)
                yield t
                cl = CTR[:, 2 * j:2 * j + 2, :, :]
                t_C[j] = low(cl, c, ch, t)
                C2[j] = ic, ch, cl
            ik, kT, f_k = yield from grab(r_kT)
            yield lambda: u in t_kw and j in t_C
            yield t_kw[u], t_C[j], f_k
            t_k1 = []
            for half in range(2):
                bi, bk, fb = yield from grab(banks)
                for c in range(2):
                    cc = 4 * u + 2 * half + c
                    for k in range(2):
                        t = mm3(bk[:, c * 256:(c + 1) * 256].rearrange("p (b t) -> p b t", b=2),
                                [w[:, k, cc * 128:(cc + 1) * 128] for w in WKV2],
                                [x[:, :, k, :] for x in C2[j][1:]],
                                k == 0, k == 1, c == 1 and k == 1, fb, t_kw[u], t_C[j])
                yield t
                t_k1.append(evac(act, kT[:, half * 512:(half + 1) * 512], bk[:, :], t, f_k))
                banks.give(bi, t_k1[-1])
            context_read(j, t)
            KS[j, u] = ik, kT, t_k1, t

        def values(b, u):
            iv, v, f_v = yield from grab(r_v)
            yield lambda: b // 2 in t_C and u in t_vw
            yield t_vw[u], t_C[b // 2], f_v
            bi, bk, fb = yield from grab(banks)
            for k in range(2):
                t = mm3(bk[:, :], [x[:, b % 2, k, :] for x in C2[b // 2][1:]],
                        [w[:, k, 1024 + u * 512:1536 + u * 512] for w in WKV2], k == 0, k == 1, k == 1,
                        fb, t_vw[u], t_C[b // 2])
            yield t
            t_v = evac(act, v, bk[:, :], t, f_v)
            banks.give(bi, t_v)
            context_read(b // 2, t)
            VS[b, u] = iv, v, t_v, t

        def attend(i, g, kT, t_kT, qT, t_q, pts, used):
            p0 = g * 64
            ism, sm, f_sm = yield from grab(r_sm1)
            ip, p, f_p = yield from grab(r_p1)
            yield t_q, t_kT
            bi, bk, f = yield from grab(banks)
            for n in range(4):
                at = n * 256 + i * 128
                t_s = mm(bk[:, n * 128:(n + 1) * 128], qT[p0:p0 + 64, at:at + 128], kT[p0:p0 + 64, at:at + 128],
                         True, True, n == 3, t_q, t_kT, f)
            used.append(t_s)
            yield t_s
            t = op(dve, partial(nc.vector.tensor_reduce, sm[:, 0:4],
                                bk[:, :].rearrange("p (n t) -> p n t", n=4), AX, ALU.max), t_s, f_sm)
            t_nm = op(dve, partial(nc.vector.tensor_scalar, sm[:, 4:8], sm[:, 0:4], -1.0, None, ALU.mult), t)
            yield t_nm
            for n in range(4):
                t_e = op(act, partial(nc.scalar.activation, p[:, n * 128:(n + 1) * 128],
                                      bk[:, n * 128:(n + 1) * 128], ACT.Exp, bias=sm[:, 4 + n:5 + n],
                                      accum_out=sm[:, 8 + n:9 + n]), t_nm, f_p)
            banks.give(bi, t_e)
            yield t_e
            t = op(dve, partial(nc.vector.reciprocal, sm[:, 12:16], sm[:, 8:12]), t_e)
            pv = p.rearrange("p (n t) -> p n t", n=4)
            t_p = op(dve, partial(nc.vector.tensor_tensor, pv, pv, sm[:, 12:16].rearrange("p (n o) -> p n o", o=1)
                                  .broadcast_to([128, 4, 128]), ALU.mult), t)
            r_sm1.give(ism, t_p)
            ipt, pt, f = yield from grab(r_pt1)
            bi, bk, t = yield from transposes(p, 4, t_p)
            r_p1.give(ip, t)
            t_pt = evac(act, pt, bk[:, :], t, f)
            banks.give(bi, t_pt)
            pts[g] = ipt, pt, t_pt

        def unit(j, u, xnT, t_n, t_xn):
            xn2 = [xnT[:, i * 512:(i + 1) * 512].rearrange("p (k t) -> p k t", k=2) for i in range(2)]
            iq, qT, f_q = yield from grab(r_qT)
            yield lambda: u in t_qw
            yield t_n, t_qw[u], f_q
            t_q = []
            for half in range(2):
                bi, bk, fb = yield from grab(banks)
                for c in range(2):
                    cc = 4 * u + 2 * half + c
                    for k in range(2):
                        t = mm3(bk[:, c * 256:(c + 1) * 256], [w[:, k, cc * 128:(cc + 1) * 128] for w in WQ2],
                                [x[:, k, :] for x in xn2], k == 0, k == 1, c == 1 and k == 1, fb, t_qw[u], t_n)
                yield t
                t_q.append(op(act, partial(nc.scalar.mul, qT[:, half * 512:(half + 1) * 512], bk[:, :], SC1), t, f_q))
                banks.give(bi, t_q[-1])
            t_xn.append(t)
            queries.append(t)
            if len(queries) == NB:
                q_free.extend(queries)
            yield lambda: (j, u) in KS
            ik, kT, t_kT, _ = KS[j, u]
            used = []
            for k in [spawn(heads(2 * j + i, i, u, kT, t_kT, qT, t_q, used)) for i in range(2)]:
                yield k
            r_kT.give(ik, used)
            r_qT.give(iq, used)
            units.append(j)
            if len(units) == NB:
                free = [kv_done, queries, list(XT.values()), [r.left for r in (r_kT, r_v, r_qT, r_p1, r_aT)]]
                t_w1.append(dma(sp, "d_wgu1", big(16, 48 * KB), a["wgu1"][:, 16 * KB:], free))
                t_wd1.append(dma(sp, "d_wd1", WD1, a["wd1"], free))

        def heads(b, i, u, kT, t_kT, qT, t_q, used):
            x = X[:, b, :]
            pts = {}
            yield t_kT, t_q
            for k in [spawn(attend(i, g, kT, t_kT, qT, t_q, pts, used)) for g in range(2)]:
                yield k
            yield lambda: (b, u) in VS
            iv, v, t_v, _ = VS[b, u]
            ia, aT, f_a = yield from grab(r_aT)
            yield pts[0][2], pts[1][2], t_v
            bi, bk, f = yield from grab(banks)
            for half in range(2):
                ipt, pt, t_pt = pts[half]
                for n in range(4):
                    t = mm(bk[half * 64:half * 64 + 64, n * 128:(n + 1) * 128],
                           v[:, (2 * n + half) * 64:(2 * n + half) * 64 + 64],
                           pt[:, n * 128:(n + 1) * 128], True, True, n == 3, t_pt, t_v, f)
                r_pt1.give(ipt, t)
            r_v.give(iv, t)
            yield t
            t_ah = high(aT[:, 0:512], bk[:, :], t, f_a)
            yield t_ah
            t_a = low(aT[:, 512:1024], bk[:, :], aT[:, 0:512], t_ah)
            banks.give(bi, t_a)
            yield lambda: bool(t_ow)
            yield t_a, t_ow
            bi, bk, f = yield from grab(banks)
            for c in range(4):
                t = mm3(bk[:, 0:D], [aT[:, i * 512 + c * 128:i * 512 + (c + 1) * 128] for i in range(2)],
                        [w[:, 4 * u + c, :] for w in WO2], c == 0, c == 3, c == 3, t_a, t_ow, f)
            r_aT.give(ia, t)
            yield t, XT[b]
            XT[b] = op(dve, partial(nc.vector.scalar_tensor_tensor, out=x, in0=bk[:, 0:D], scalar=tg[:, 0:1], in1=x,
                                    op0=ALU.mult, op1=ALU.add), t, XT[b], t_tg)
            banks.give(bi, XT[b])

        def prologue(b, xnT, f_n, t_n):
            x = X[:, b, :]
            yield lambda: b < 2 or b - 2 in XT
            got = yield from gathered(R0, b, ys0)
            t_x = combine(R0, b, got, res_done[b])
            i_s, sx, t = yield from twice_normal(x, t_x)
            ixn, xn, f = yield from grab(r_xn)
            t_xn = op(dve, partial(nc.vector.tensor_scalar, xn, x, sx[:, 6:7], sx[:, 9:10], ALU.subtract, ALU.mult), t, f)
            stat.give(i_s, t_xn)
            XT[b] = op(pool, partial(nc.gpsimd.tensor_tensor, x, x, btg[:, :], ALU.add), t_x, t_xn, t_btg)
            ixf, xf, f = yield from grab(r_xf)
            bi, bk, t = yield from transposes(xn, 2, t_xn)
            r_xn.give(ixn, t)
            for k in range(2):
                t = op(dve, partial(nc.vector.tensor_scalar, xf[:, k * 128:(k + 1) * 128],
                                    bk[:, k * 128:(k + 1) * 128], gam[:, k:k + 1], bet[:, k:k + 1],
                                    ALU.mult, ALU.add), t, f, t_s1)
            banks.give(bi, t)
            yield t
            hi, lo = (xnT[:, i * 512:(i + 1) * 512].rearrange("p (k b t) -> p k b t", k=2, b=2)[:, :, b % 2, :]
                      for i in range(2))
            xf = xf.rearrange("p (k t) -> p k t", k=2)
            t = high(hi, xf, t, f_n)
            yield t
            t_n.append(low(lo, xf, hi, t))
            normal.add(b)
            r_xf.give(ixf, t_n[-1])

        def cross_pair(j):
            iT, xnT, f = yield from grab(r_xnT)
            t_n, t_xn = [], []
            for k in [spawn(prologue(2 * j + i, xnT, f, t_n)) for i in range(2)]:
                yield k
            for k in [spawn(unit(j, u, xnT, t_n, t_xn)) for u in range(2)]:
                yield k
            r_xnT.give(iT, t_xn)
            for k in [spawn(epilogue(2 * j + i)) for i in range(2)]:
                yield k

        def epilogue(b):
            x = X[:, b, :]
            itt, tt, f = yield from grab(r_tt)
            t_tt = yield from layernorm(x, tt[:, :], XT[b], f)
            x4[b] = t_tt
            bi, bk, t = yield from transposes(tt, 2, t_tt)
            hT = CT[:, b, :, :].rearrange("p k t -> p (k t)")
            t_hT[b] = evac(act, hT, bk[:, 0:D], t, [KS[b // 2, u][-1] for u in range(2)],
                           [VS[b // 2 * 2 + i, u][-1] for i in range(2) for u in range(2)])
            t_ttpe = t
            banks.give(bi, t_hT[b])
            yield t_hT[b]
            bi, bk, f = yield from grab(banks)
            for k in range(2):
                t = mm(bk[:, 0:E1], CT[:, b, k, :], rt1[:, k, :], k == 0, k == 1, k == 1, t_hT[b], t_s1, f)
            t_log1[b] = t
            t_sc = yield from route_tile(R1, b, (bi, bk), t, itt, tt, t_tt)
            r_tt.give(itt, t_sc, t_ttpe)

        WSG = big(104, 8 * KB, pat="p (k n) -> p k n", k=2)
        WSG2 = [big(at, 8 * KB, r=True, pat="p (k n) -> p k n", k=2) for at in (96, 104)]
        WSD = big(112, 4 * KB, pat="p (c n) -> p c n", c=4)
        r_hs = Ring([small[:, 0:1024]], [end0])
        r_xh = Ring([big(at, 512, r=True) for at in (116, 118)])
        t_sw = []

        def shared_weights():
            yield lambda: bool(q_free)
            yield t_ws, q_free
            t = []
            for lo in range(0, 1024, 512):
                t.append((yield from parts(WSG2, WSG, lo, lo + 512, [t_ws, q_free])))
            t_sw.extend(t)

        def routing():
            yield lambda: len(R1.pf) == NB
            yield R1.cnt
            R1.pad, R1.y1, R1.tifree = PADI[:, :], Y1[:, :], [R0.tpad, xs0, end1]
            R1.ohw, R1.ohwfree = big(152, 2 * NB * E1, pat="p (a n) -> p a n", n=E1), end1
            R1.yifree = [(f"d_g{i}", sem(f"d_g{i}")[1]) for i in range(2)]
            route_end(R1, (sp, sp))
            R1.gwfree = list(XT.values())
            R1.gw = gates(R1, True)

        XP = {}

        def split(j):
            pair = 2 * j, 2 * j + 1
            yield lambda: bool(t_ws) and all(b in t_log1 for b in pair)
            ix, xh, f = yield from grab(r_xh)
            c = CT[:, 2 * j:2 * j + 2, :, :]
            xh = xh.rearrange("p (b k t) -> p b k t", b=2, k=2)
            xl = CTR[:, 2 * j:2 * j + 2, :, :]
            t = [t_hT[b] for b in pair]
            yield t
            t = high(xh, c, t, f)
            yield t
            XP[j] = ix, xh, xl, low(xl, c, xh, t, [t_log1[b] for b in pair])

        def shared(j):
            ih, hs, f_h = yield from grab(r_hs)
            yield lambda: bool(t_sw) and j in XP
            ix, xh, xl, t_xl = XP[j]
            ready = [t_ws, t_sw, t_xl]
            th = []
            for c in range(0, 4, 2):
                yield ready
                ig, gk, f1 = yield from grab(banks)
                iu, uk, f2 = yield from grab(banks)
                for o_, w0, fb in ((gk, 0, f1), (uk, 512, f2)):
                    for i in range(2):
                        at = w0 + (c + i) * 128
                        for k in range(2):
                            t = mm3(o_[:, i * 256:(i + 1) * 256].rearrange("p (b t) -> p b t", b=2),
                                    [w[:, k, at:at + 128] for w in WSG2], [x[:, :, k, :] for x in (xh, xl)],
                                    k == 0, k == 1, i == 1 and k == 1, fb, ready)
                    if w0 == 0:
                        t_g = t
                h = hs[:, c * 256:(c + 2) * 256]
                yield t_g
                t_sg = op(act, partial(nc.scalar.activation, h, gk[:, :], ACT.Silu), t_g, f_h)
                banks.give(ig, t_sg)
                yield t, t_sg
                th.append(op(dve, partial(nc.vector.tensor_tensor, h, uk[:, :], h, ALU.mult), t, t_sg))
                banks.give(iu, th[-1])
            r_xh.give(ix, t)
            yield th
            for i in range(2):
                b = 2 * j + i
                bi, bk, f = yield from grab(banks)
                for c in range(4):
                    t = mm(bk[:, 0:D], hs[:, c * 256 + i * 128:c * 256 + (i + 1) * 128], WSD[:, c, :], c == 0, c == 3,
                           c == 3, th, f)
                yield t
                x4[b] = op(dve, partial(nc.vector.tensor_tensor, X[:, b, :], bk[:, 0:D], X[:, b, :], ALU.add), t, x4[b])
                banks.give(bi, x4[b])
            r_hs.give(ih, t)

        EARLY, NEXT, AHEAD = 3, 5, 2
        weave.run((g for j in range(-1, NB // 2 + 1)
                   for g in ((weights(), shared_weights(), routing()) if j < 0 else [split(i) for i in range(EARLY + AHEAD)] + [shared(i) for i in range(EARLY)] if j == NB // 2 else (*(g(*at) for u in range(2) for g, at in ((keys, (j, u)), (values, (2 * j, u)),
                                                                      (values, (2 * j + 1, u)))), cross_pair(j)))),
                  24, 50.0)
        end2 = now()
        r_hs.tiles.append(big(148, 1024))
        r_hs.left.append(end2)
        r_hs.free.append(1)

        ring = space((120, 148))
        rings1 = [ring(2, 4 * F1, end2), ring(2, 4 * F1, end2, r=True), ring(3, D, end2), ring(2, D, end2),
                  ring(2, F1, end2), ring(1, 2 * F1, end2, r=True), ring(2, D, end2)]
        R1.ysfree = [(f"d_g{i}", sem(f"d_g{i}")[1]) for i in range(2)]
        done1 = {}
        experts(R1, rings1, WGU1, WD1, F1, t_w1, t_wd1, done1, others=[split(j) for j in range(EARLY + AHEAD, NEXT)] + [shared(j) for j in range(EARLY, NEXT)])
        G[0] = Ring([big(2 * i, 512) for i in range(NB)], now())
        ys1 = list(done1.values())

        outs, left = [], dict.fromkeys(range(NB), 1)
        left.update(dict.fromkeys(range(2 * NEXT, NB), 2))

        def finished(b):
            left[b] -= 1
            if not left[b]:
                yield x4[b]
                outs.append(dma(sp, "d_out", out[b], X[:, b, :], x4[b]))

        def last(b):
            got = yield from gathered(R1, b, ys1)
            x4[b] = combine(R1, b, got, x4[b])
            yield from finished(b)

        def shared_last(j):
            yield from shared(j)
            for b in (2 * j, 2 * j + 1):
                yield from finished(b)

        weave.run([split(j) for j in range(max(NEXT, EARLY + AHEAD), NB // 2)] + [shared_last(j) for j in range(NEXT, NB // 2)]
                  + [last(b) for b in (*range(2 * NEXT, NB), *range(2 * NEXT))], NB + 6, 0.0)
        quiet(sp, lambda e: e.nop(), outs[-1])

        block = ctx.enter_context(nc.Block())

        @block.sync
        def _(e):
            play(sp, e)

        @block.gpsimd
        def _(e):
            play(pool, e)

        @block.vector
        def _(e):
            play(dve, e)

        @block.scalar
        def _(e):
            play(act, e)

        @block.tensor
        def _(e):
            play(pe, e)


def laid_out(i):
    def kp(w):
        k, n = w.shape
        return w.reshape(k // 128, 128, n).transpose(1, 0, 2).reshape(128, -1)

    def ekp(w):
        e, k, n = w.shape
        return w.reshape(e, k // 128, 128, n).transpose(2, 0, 1, 3).reshape(128, -1)

    def rows(v):
        return np.broadcast_to(v.reshape(1, -1), (128, v.size))

    def cols(v):
        return v.reshape(-1, 128).T

    cat = np.concatenate
    d = {
        "consts": constants(),
        "x": i["x"],
        "ctxT": i["ctx_1024"].reshape(NB, 128, 2, 128).transpose(3, 0, 2, 1),
        "small0": cat([kp(i["L0_ffn_w_down"]), i["L0_ffn_wq"], i["L0_ffn_wk"], i["L0_ffn_wv"], i["L0_ffn_w_up"],
                       kp(i["L0_ffn_router_w"]), rows(i["L0_ffn_g2"]), cols(i["L0_ffn_g1"])], axis=1),
        "wgu0": ekp(cat([i["L0_ffn_w1"], i["L0_ffn_w3"]], axis=2)),
        "wd0": ekp(i["L0_ffn_w2"]),
        "wq1": kp(i["L1_xattn_w_q"]),
        "wkv1": kp(i["L1_xattn_w_kv"]),
        "wo1": kp(i["L1_xattn_w_out"]),
        "small1": cat([cols(i["L1_xattn_ln_gamma"]), cols(i["L1_xattn_ln_beta"]), rows(i["L1_xattn_b_out"]),
                       rows(i["L1_xattn_gate"]), kp(i["L1_ffn_router_w"].T)], axis=1),
        "wgu1": ekp(i["L1_ffn_gate_up_w"]),
        "wd1": ekp(i["L1_ffn_down_w"]),
        "wsgu": kp(cat([i["L1_ffn_shared_gate_w"].T, i["L1_ffn_shared_up_w"].T], axis=1)),
        "wsd": kp(i["L1_ffn_shared_down_w"].T),
    }
    return {k: np.ascontiguousarray(v) for k, v in d.items()}


def kernel(**inputs):
    import concourse.bacc as _bacc
    from concourse.bass_utils import run_bass_kernel_spmd as _run

    arrays = laid_out({k: np.asarray(v) for k, v in inputs.items()})
    nc = _bacc.Bacc("TRN2", target_bir_lowering=False, num_devices=1)
    args = {k: nc.dram_tensor(f"in_{k}", v.shape, mybir.dt.from_np(v.dtype), kind="ExternalInput").ap()
            for k, v in arrays.items()}
    out = nc.dram_tensor("out_dram", (NB, 128, D), F32, kind="ExternalOutput").ap()
    program(nc, args, out)
    r = _run(nc, [{f"in_{k}": v for k, v in arrays.items()}], core_ids=[0])
    return r.results[0]["out_dram"]
```
